# Optimizing a Trainium2 kernel written in Bass

```python
import numpy as np
import jax
import jax.numpy as jnp

def _softmax(x, axis=-1):
    return jax.nn.softmax(x, axis=axis)

def _gelu(x):
    return jax.nn.gelu(x, approximate=True)

def _silu(x):
    return jax.nn.silu(x)

def _sigmoid(x):
    return jax.nn.sigmoid(x)

def _layernorm(x, axis=-1, eps=1e-05):
    m = jnp.mean(x, axis=axis, keepdims=True)
    v = jnp.var(x, axis=axis, keepdims=True)
    return (x - m) / jnp.sqrt(v + eps)

def _scatter_add(tgt, idx, src, axis=0):
    return tgt.at[idx].add(src)

def _segment_sum(src, seg, n):
    return jax.ops.segment_sum(src, seg, n)
kernel_name = 'mk_macaron_d1_jaxref_r8_ae3534'

def setup_inputs(seed: int=0):
    np.random.seed(seed)
    _w = jnp.asarray

    def _L0_attn_setup():
        import jax, jax.numpy as jnp
        import numpy as np
        import math
        DIM = 128
        NUM_HEADS = 16
        HEAD_DIM = DIM // NUM_HEADS
        BATCH = 4
        SEQ = 512

        def _feature_map(x, R):
            x = x / math.sqrt(HEAD_DIM)
            proj = jnp.einsum('bhnd,dm->bhnm', x, R)
            sq_norm = jnp.sum(x * x, axis=-1, keepdims=True)
            return jnp.exp(proj - 0.5 * sq_norm)
        key = jax.random.key(seed)
        ks = jax.random.split(key, 10)
        s = 1.0 / math.sqrt(DIM)
        return {'x': jax.random.normal(ks[0], (BATCH, SEQ, DIM), dtype=jnp.float32), 'Wq': jax.random.normal(ks[1], (DIM, DIM), dtype=jnp.float32) * s, 'bq': jax.random.normal(ks[2], (DIM,), dtype=jnp.float32) * 0.01, 'Wk': jax.random.normal(ks[3], (DIM, DIM), dtype=jnp.float32) * s, 'bk': jax.random.normal(ks[4], (DIM,), dtype=jnp.float32) * 0.01, 'Wv': jax.random.normal(ks[5], (DIM, DIM), dtype=jnp.float32) * s, 'bv': jax.random.normal(ks[6], (DIM,), dtype=jnp.float32) * 0.01, 'Wo': jax.random.normal(ks[7], (DIM, DIM), dtype=jnp.float32) * s, 'bo': jax.random.normal(ks[8], (DIM,), dtype=jnp.float32) * 0.01, 'R': jax.random.normal(ks[9], (HEAD_DIM, HEAD_DIM), dtype=jnp.float32) * 0.4}
    _L0_attn_in = _L0_attn_setup()

    def _L0_ffn_setup():
        import jax, jax.numpy as jnp
        import numpy as np
        LORA_DIM = 16
        LORA_TOKEN_INDEX = 1
        B, S, D, H = (4, 256, 128, 512)
        key = jax.random.key(seed)
        ks = jax.random.split(key, 6)
        x = jax.random.normal(ks[0], (B, S, D), dtype=jnp.float32)
        W1 = jax.random.normal(ks[1], (H, D), dtype=jnp.float32) * 0.02
        b1 = jnp.zeros((H,), dtype=jnp.float32)
        W2 = jax.random.normal(ks[2], (D, H), dtype=jnp.float32) * 0.02
        b2 = jnp.zeros((D,), dtype=jnp.float32)
        scale = jnp.asarray(0.001, dtype=jnp.float32)
        return {'x': x, 'W1': W1, 'b1': b1, 'W2': W2, 'b2': b2, 'scale': scale}
    _L0_ffn_in = _L0_ffn_setup()
    _d = {'L0_attn_x': _L0_attn_in['x'], 'L0_attn_Wq': _L0_attn_in['Wq'], 'L0_attn_bq': _L0_attn_in['bq'], 'L0_attn_Wk': _L0_attn_in['Wk'], 'L0_attn_bk': _L0_attn_in['bk'], 'L0_attn_Wv': _L0_attn_in['Wv'], 'L0_attn_bv': _L0_attn_in['bv'], 'L0_attn_Wo': _L0_attn_in['Wo'], 'L0_attn_bo': _L0_attn_in['bo'], 'L0_attn_R': _L0_attn_in['R'], 'L0_ffn_W1': _L0_ffn_in['W1'], 'L0_ffn_b1': _L0_ffn_in['b1'], 'L0_ffn_W2': _L0_ffn_in['W2'], 'L0_ffn_b2': _L0_ffn_in['b2'], 'L0_ffn_scale': _L0_ffn_in['scale']}
    _x0 = _d['L0_attn_x']
    _d['L0_attn_x'] = jax.random.normal(jax.random.fold_in(jax.random.key(seed), 1), (4, 1024, 128), dtype=_x0.dtype)
    del _x0
    return _d

def reference(L0_attn_x, L0_attn_Wq, L0_attn_bq, L0_attn_Wk, L0_attn_bk, L0_attn_Wv, L0_attn_bv, L0_attn_Wo, L0_attn_bo, L0_attn_R, L0_ffn_W1, L0_ffn_b1, L0_ffn_W2, L0_ffn_b2, L0_ffn_scale):

    def _L0_attn_ref(x, Wq, bq, Wk, bk, Wv, bv, Wo, bo, R):
        import jax, jax.numpy as jnp
        import numpy as np
        import math
        DIM = 128
        NUM_HEADS = 16
        HEAD_DIM = DIM // NUM_HEADS
        BATCH = 4
        SEQ = 512

        def _feature_map(x, R):
            x = x / math.sqrt(HEAD_DIM)
            proj = jnp.einsum('bhnd,dm->bhnm', x, R)
            sq_norm = jnp.sum(x * x, axis=-1, keepdims=True)
            return jnp.exp(proj - 0.5 * sq_norm)
        b, n, _ = x.shape
        h, d = (NUM_HEADS, HEAD_DIM)

        def split_heads(t):
            return t.reshape(b, n, h, d).transpose(0, 2, 1, 3)
        q = split_heads(x @ Wq.T + bq)
        k = split_heads(x @ Wk.T + bk)
        v = split_heads(x @ Wv.T + bv)
        q_prime = _feature_map(q, R)
        k_prime = _feature_map(k, R)
        kv = jnp.einsum('bhnd,bhne->bhde', k_prime, v)
        z = 1.0 / (jnp.sum(q_prime, axis=-1) + 1e-08)
        out = jnp.einsum('bhnd,bhde,bhn->bhne', q_prime, kv, z)
        out = out.transpose(0, 2, 1, 3).reshape(b, n, DIM)
        return out @ Wo.T + bo

    def _L0_ffn_ref(x, W1, b1, W2, b2, scale):
        import jax, jax.numpy as jnp
        import numpy as np
        LORA_DIM = 16
        LORA_TOKEN_INDEX = 1
        B, S, D, H = (4, 256, 128, 512)
        Bx, Sx, Dx = x.shape
        Hx = W1.shape[0]
        lt = jax.lax.dynamic_slice_in_dim(x, LORA_TOKEN_INDEX, LORA_DIM, axis=1)
        even = lt[:, ::2, :]
        odd = lt[:, 1::2, :]
        m1 = (even[:, :4, :, None] * odd[:, :4, None, :]).reshape(Bx, Hx, Dx)
        m2 = (even[:, 4:, :, None] * odd[:, 4:, None, :]).reshape(Bx, Dx, Hx)
        h = jnp.einsum('bsd,hd->bsh', x, W1) + scale * jnp.einsum('bsd,bhd->bsh', x, m1) + b1
        h = jax.nn.gelu(h, approximate=False)
        out = jnp.einsum('bsh,oh->bso', h, W2) + scale * jnp.einsum('bsh,boh->bso', h, m2) + b2
        return out
    x = L0_attn_x
    x = x + 0.5 * _L0_ffn_ref(_layernorm(x, axis=-1), L0_ffn_W1, L0_ffn_b1, L0_ffn_W2, L0_ffn_b2, L0_ffn_scale)
    x = x + _L0_attn_ref(_layernorm(x, axis=-1), L0_attn_Wq, L0_attn_bq, L0_attn_Wk, L0_attn_bk, L0_attn_Wv, L0_attn_bv, L0_attn_Wo, L0_attn_bo, L0_attn_R)
    x = x + 0.5 * _L0_ffn_ref(_layernorm(x, axis=-1), L0_ffn_W1, L0_ffn_b1, L0_ffn_W2, L0_ffn_b2, L0_ffn_scale)
    return x

_drawn_inputs = setup_inputs


def setup_inputs(seed=0):
    import zlib

    import numpy as np

    out = dict(_drawn_inputs(seed))
    spreads = {'L0_ffn_b1': (0.0, 0.1), 'L0_ffn_b2': (0.0, 0.1)}
    factors = {'L0_attn_bq': 37.169, 'L0_attn_bk': 8.0, 'L0_attn_bo': 200.0, 'L0_ffn_W1': 2.736}
    for name, (base, spread) in spreads.items():
        noise = np.random.default_rng([zlib.crc32(name.encode()), seed]).standard_normal(out[name].shape)
        drawn = base * np.exp(spread * noise) if base else spread * noise
        out[name] = jnp.asarray(drawn.astype(out[name].dtype))
    for name, factor in factors.items():
        out[name] = (out[name] * factor).astype(out[name].dtype)
    return out
```

```python
import numpy as np
from contextlib import ExitStack

import concourse.bass as bass
from concourse import mybir

ALU = mybir.AluOpType
ACT = mybir.ActivationFunctionType
AX = mybir.AxisListType
F32 = mybir.dt.float32
F32R = mybir.dt.float32r

P = 128
D = 128
H = 512
NB, SEQ = 4, 1024
HEADS, HD = 16, 8
TOK = 512
NT = TOK // P
CHUNKS = NB * SEQ // TOK
PER_B = SEQ // TOK
HB = H // P
LORA = 4
LN_EPS, Z_EPS = 1e-5, 1e-8
NG = 3 * CHUNKS


def build(nc, x, wq, bq, wk, bk, wv, bv, wo, bo, r, w1, b1, w2, b2, scale, out, rows_dram):
    ctx = ExitStack()
    with ctx:
        def sb(name, shape, dt=F32):
            return ctx.enter_context(nc.sbuf_tensor(name, shape, dt))

        def sem(name):
            return ctx.enter_context(nc.semaphore(name))

        X = sb("X", [P, NG, NT, D])
        xn = sb("xn", [P, 6, NT, D + 2])
        mv = sb("mv", [P, 2, NT, 2])
        bst = sb("bst", [P, 2, NT, 6])
        veps = sb("veps", [P, 2, NT])
        rstd = sb("rstd", [P, 2, NT])
        mhalf = sb("mhalf", [P, NT])
        xh = sb("xh", [P, 2, TOK], F32R)
        xl = sb("xl", [P, 2, TOK], F32R)
        gl = sb("gl", [P, 2, HB, TOK])
        w1n = sb("w1n", [P, HB, D])
        w2n = sb("w2n", [P, H])
        w1t = sb("w1t", [P, H])
        w2t = sb("w2t", [P, HB, D])
        ev = sb("ev", [P, 2 * LORA, D])
        od = sb("od", [P, 2 * LORA])
        scl = sb("scl", [P, 2 * LORA])
        w1r = sb("w1r", [P, LORA, D])
        w1h = sb("w1h", [P, H], F32R)
        w1l = sb("w1l", [P, H], F32R)
        w2m = sb("w2m", [P, LORA, D])
        w2e = sb("w2e", [P, HB, D])
        brows = sb("brows", [HB + 4, P])
        bcol = sb("bcol", [P, HB + 4])
        b2b = sb("b2b", [P, D])
        bob = sb("bob", [P, D])
        bvb = sb("bvb", [P, D])
        scb = sb("scb", [P, 1])
        ident = sb("ident", [P, P])
        bd = sb("bd", [P, HEADS, HD])
        rrep = sb("rrep", [P, HD])
        rbd = sb("rbd", [P, P])
        wn = sb("wn", [P, 4, D])
        wah = sb("wah", [P, TOK], F32R)
        wal = sb("wal", [P, TOK], F32R)
        bhi = sb("bhi", [2, TOK], F32R)
        brow = sb("brow", [P, TOK], F32R)
        ones = sb("ones", [P, P], F32R)
        negm = sb("negm", [2, 1])
        wvo = sb("wvo", [P, 2, D])
        sq = sb("sq", [P, 2, 4, P])
        s8 = sb("s8", [P, 2, 4 * HEADS])
        ex = sb("ex", [P, 2, 4, P])
        qk = sb("qk", [P, 2, NT, 2, P])
        zs = sb("zs", [P, 3, NT * HEADS])
        zr = sb("zr", [P, NT, HEADS])
        qn = sb("qn", [P, NT, P])
        qt = sb("qt", [P, 4, TOK])
        gs = sb("gs", [P, D + 2])
        gt = sb("gt", [P, D])
        kvb = sb("kvb", [P, D])
        kvm = sb("kvm", [P, D])
        kvt = sb("kvt", [P, D])
        mo = sb("mo", [P, D])

        bank = [ctx.enter_context(nc.psum_tensor(f"bank{i}", [P, TOK], F32)) for i in range(1)]
        quad = ctx.enter_context(nc.psum_tensor("quad", [P, 4, TOK], F32))
        bank += [quad[:, i, :] for i in range(4)]
        bank += [ctx.enter_context(nc.psum_tensor(f"bank{i}", [P, TOK], F32)) for i in range(5, 8)]
        ps_t, ps_h, ps_y = bank[0], bank[1:3], bank[3:5]
        ps_g, ps_r, ps_m = bank[5], bank[6], bank[7]
        ps_o = [ps_m, ps_r]

        ld_x = [sem(f"ld_x{c}") for c in range(CHUNKS)]
        ld_w1, ld_w2, ld_f, ld_a = sem("ld_w1"), sem("ld_w2"), sem("ld_f"), sem("ld_a")
        k_id, k_bd, k_exp, k_ones = sem("k_id"), sem("k_bd"), sem("k_exp"), sem("k_ones")
        k_neg, k_brow, k_col = sem("k_neg"), sem("k_brow"), sem("k_col")
        k_pool = sem("k_pool")
        w1t_ps, w2t_ps, w1t_in, w2t_in = sem("w1t_ps"), sem("w2t_ps"), sem("w1t_in"), sem("w2t_in")
        scl_in, bcol_ps, bcol_in = sem("scl_in"), sem("bcol_ps"), sem("bcol_in")
        rbd_in, att_ps, wah_in, wal_in = sem("rbd_in"), sem("att_ps"), sem("wah_in"), sem("wal_in")
        wvo_in, bhi_in, brow_in = sem("wvo_in"), sem("bhi_in"), sem("brow_in")
        s_bst, s_mv, s_veps = sem("s_bst"), sem("s_mv"), sem("s_veps")
        s_rstd, s_xn, s_xt = sem("s_rstd"), sem("s_xn"), sem("s_xt")
        s_hi, s_lo, s_xb, s_x = sem("s_hi"), sem("s_lo"), sem("s_xb"), sem("s_x")
        s_rows, s_ev = sem("s_rows"), sem("s_ev")
        s_od, s_w1r, s_w1h, s_w1 = sem("s_od"), sem("s_w1r"), sem("s_w1h"), sem("s_w1")
        s_w2m, s_w2 = sem("s_w2m"), sem("s_w2")
        s_u, s_gelu, s_d = sem("s_u"), sem("s_gelu"), sem("s_d")
        s_qk, s_sq, s_red, s_sub, s_exp = sem("s_qk"), sem("s_sq"), sem("s_red"), sem("s_sub"), sem("s_exp")
        s_zs, s_ze, s_zr, s_qn, s_qt = sem("s_zs"), sem("s_ze"), sem("s_zr"), sem("s_qn"), sem("s_qt")
        s_qte, s_g, s_o = sem("s_qte"), sem("s_g"), sem("s_o")
        s_gs, s_gtp, s_gt, s_kv, s_kvb = sem("s_gs"), sem("s_gtp"), sem("s_gt"), sem("s_kv"), sem("s_kvb")
        s_kvm, s_ktp, s_kt, s_mp, s_mo = sem("s_kvm"), sem("s_ktp"), sem("s_kt"), sem("s_mp"), sem("s_mo")
        s_out = sem("s_out")

        def chunk_of(t, c):
            flat = t.rearrange("b s d -> (b s) d")
            return flat[c * TOK:(c + 1) * TOK, :].rearrange("(n p) d -> p n d", p=P)

        def wait(eng, s, n):
            if not isinstance(n, int) or n > 0:
                eng.wait_ge(s, n)

        def slot(g):
            return g % 2 if g < CHUNKS or g >= 2 * CHUNKS else 2 + g % 4

        def f_of(g):
            return g if g < CHUNKS else g - CHUNKS

        def is_ffn(g):
            return g < CHUNKS or g >= 2 * CHUNKS

        def plan():
            yield "setup", 0
            yield "stats", 0
            yield "norm", 0
            yield "rows", 0
            yield "stats", 1
            yield "turn", 0
            yield "norm", 1
            yield "w1", 0
            yield "w2mul", 0
            yield "w2add", 0
            for s in range(NG):
                if s + 2 < NG:
                    yield "stats", s + 2
                if s + 1 < NG:
                    yield "turn", s + 1
                if is_ffn(s):
                    f = f_of(s)
                    yield "up", f
                    if s + 2 < NG:
                        yield "norm", s + 2
                        if is_ffn(s + 2) and s % PER_B == 0:
                            yield "rows", f_of(s + 2) // PER_B
                    if s == 1:
                        yield "setup_att", 0
                    if s % PER_B == 1 and s + 1 < NG and is_ffn(s + 1):
                        yield "w1", f_of(s + 1) // PER_B
                        yield "w2mul", f_of(s + 1) // PER_B
                    if s == 2 * CHUNKS:
                        yield "qturn", CHUNKS - 1
                        yield "gram", CHUNKS - 1
                    if s == 2 * CHUNKS + 1:
                        for k in range(4):
                            yield "mix", (NB - 1, k)
                        yield "o", (NB - 1, 0)
                        yield "o", (NB - 1, 1)
                    if s not in (0, 2 * CHUNKS):
                        yield "down", f - 1
                    if s % PER_B == 0 and s > 0:
                        yield "w2add", f // PER_B
                    if s == NG - 1:
                        yield "down", f
                else:
                    a = s - CHUNKS
                    mixing = a % PER_B == 1 and a >= 3
                    for n in range(NT):
                        if a == 0 and n == 2:
                            yield "down", CHUNKS - 1
                        yield "qk", (a, n)
                        if mixing:
                            yield "mix", (a // PER_B - 1, n)
                        if n % 2 == 1:
                            yield "feat", (a, n // 2)
                    yield "norm", s + 2
                    if s == 2 * CHUNKS - 2:
                        yield "rows", NB
                    if a > 0:
                        yield "qturn", a - 1
                        yield "gram", a - 1
                    yield "z", a
                    if mixing:
                        yield "o", (a // PER_B - 1, 0)
                        yield "o", (a // PER_B - 1, 1)
                    if s == 2 * CHUNKS - 1:
                        yield "w1", NB
                        yield "w2mul", NB

        def store(sp, g):
            sp.wait_ge(s_x, g + 1)
            sp.dma_start(chunk_of(out, g - 2 * CHUNKS), X[:, g]).then_inc(s_out, 16)

        def pool_late_constants(pool):
            n = 1
            pool.memset(bd[:], 1.0).then_inc(k_pool, 1)
            n += 1
            pool.wait_ge(k_pool, n)
            pool.affine_select(out=bd[:], in_=bd[:], compare_op=ALU.is_ge, fill=0.0, base=0,
                               pattern=[[-HD, HEADS], [0, HD]], channel_multiplier=1).then_inc(k_pool, 1)
            n += 1
            pool.wait_ge(k_pool, n)
            pool.affine_select(out=bd[:], in_=bd[:], compare_op=ALU.is_ge, fill=0.0, base=HD - 1,
                               pattern=[[HD, HEADS], [0, HD]], channel_multiplier=-1).then_inc(k_bd, 1)
            pool.memset(negm[:], -1.0).then_inc(k_pool, 1)
            n += 1
            pool.wait_ge(k_pool, n)
            pool.affine_select(out=negm[:], in_=negm[:], compare_op=ALU.is_gt, fill=0.0, base=0,
                               pattern=[[0, 1]], channel_multiplier=1).then_inc(k_neg, 1)
            pool.memset(brow[:].bitcast(F32), 0.0).then_inc(k_brow, 1)
            pool.memset(ones[:].bitcast(F32), 1.0).then_inc(k_ones, 1)
            pool.memset(xn[:, :, :, D:D + 2], 1.0).then_inc(k_col, 1)

        def halves(p, which):
            return quad[:, 2 * p:2 * p + 2, :].rearrange("p n (k w d) -> p w (n k) d", k=2, w=2)[:, which]

        def wait_xhl(eng, g):
            if g >= 2:
                if is_ffn(g - 2):
                    eng.wait_ge(s_u, HB * (f_of(g - 2) + 1))
                else:
                    eng.wait_ge(s_qk, NT * (g - 2 - CHUNKS + 1))

        def add(dve, g, product):
            dve.wait_ge(s_xb, g + 1)
            to = g + CHUNKS if g < 2 * CHUNKS else g
            dve.tensor_tensor(X[:, to].rearrange("p n d -> p (n d)"), product[:],
                              X[:, g].rearrange("p n d -> p (n d)"), ALU.add).then_inc(s_x, 1)

        block = ctx.enter_context(nc.Block())

        @block.sync
        def _(sp):
            for c in range(CHUNKS):
                sp.dma_start(X[:, c], chunk_of(x, c)).then_inc(ld_x[c], 16)
            for stage, i in plan():
                if stage == "rows":
                    g = i * PER_B if i < NB else i * PER_B + CHUNKS
                    sp.wait_ge(s_xn, g + 1)
                    sp.dma_start(rows_dram[i], xn[1:1 + 4 * LORA, slot(g), 0, 0:D]).then_inc(s_rows, 16)
                    sp.wait_ge(s_rows, 16 * (i + 1))
                    wait(sp, s_w1r, i)
                    wait(sp, s_w2m, i)
                    even = rows_dram[i].rearrange("(n two) d -> two n d", two=2)[0]
                    sp.dma_start(ev[:], even.partition_broadcast(P)).then_inc(s_ev, 16)
                if stage == "down" and i > CHUNKS:
                    store(sp, i + CHUNKS - 1)
            store(sp, NG - 1)
            sp.wait_ge(s_out, 16 * CHUNKS)

        @block.gpsimd
        def _(pool):
            pool.memset(mhalf[:], -0.5).then_inc(k_exp, 1)
            pool.memset(ident[:], 0.0).then_inc(k_pool, 1)
            pool.wait_ge(k_pool, 1)
            pool.affine_select(out=ident[:], in_=ident[:], compare_op=ALU.not_equal, fill=1.0, base=0,
                               pattern=[[-1, P]], channel_multiplier=1).then_inc(k_id, 1)
            for stage, i in plan():
                if stage == "stats":
                    pool.wait_ge(s_veps, i + 1)
                    if i == 0:
                        pool.wait_ge(k_exp, 1)
                    wait(pool, s_xn, i - 1)
                    pool.tensor_tensor(rstd[:, i % 2], veps[:, i % 2], mhalf[:], ALU.pow).then_inc(s_rstd, 1)
                if stage == "norm":
                    if i == 1:
                        pool_late_constants(pool)
                    pool.wait_ge(s_xn, i + 1)
                    if i == 0:
                        pool.wait_ge(scl_in, 1)
                    if i == CHUNKS:
                        pool.wait_ge(ld_a, 16 * 7)
                    bias = b2b if is_ffn(i) else bob
                    pool.tensor_tensor(X[:, i], X[:, i], bias[:].unsqueeze(1).to_broadcast([P, NT, D]),
                                       ALU.add).then_inc(s_xb, 1)
                if stage == "w2mul":
                    pool.wait_ge(s_ev, 16 * (i + 1))
                    pool.wait_ge(s_od, i + 1)
                    wait(pool, s_w2, i)
                    pool.tensor_tensor(w2m[:], ev[:, LORA:2 * LORA],
                                       od[:, LORA:2 * LORA].unsqueeze(2).to_broadcast([P, LORA, D]),
                                       ALU.mult).then_inc(s_w2m, 1)
                if stage == "w2add":
                    pool.wait_ge(s_w2m, i + 1)
                    pool.wait_ge(w2t_in, 1)
                    wait(pool, s_d, PER_B * i)
                    pool.tensor_tensor(w2e[:], w2m[:].rearrange("p i d -> p (i d)").rearrange("p (o k) -> p k o", k=HB),
                                       w2t[:], ALU.add).then_inc(s_w2, 1)
                if stage == "z":
                    pool.wait_ge(s_zr, i + 1)
                    wait(pool, s_qt, i)
                    pool.tensor_tensor(qn[:].rearrange("p n (h d) -> p n h d", h=HEADS),
                                       qk[:, i % 2, :, 0, :].rearrange("p n (h d) -> p n h d", h=HEADS),
                                       zr[:].unsqueeze(3).to_broadcast([P, NT, HEADS, HD]),
                                       ALU.mult).then_inc(s_qn, 1)

        @block.scalar
        def _(act):
            act.dma_start(w1n[:], w1.rearrange("(j p) d -> p j d", p=P)).then_inc(ld_w1, 16)
            act.dma_start(w2n[:], w2).then_inc(ld_w2, 16)
            act.dma_start(scb[:], scale.partition_broadcast(P)).then_inc(ld_f, 16)
            act.dma_start(brows[0:HB, :], b1.rearrange("(j p) -> j p", p=P)).then_inc(ld_f, 16)
            for k, v in enumerate((bq, bk)):
                act.dma_start(brows[HB + 2 * k:HB + 2 * k + 2, :], v.partition_broadcast(2)).then_inc(ld_f, 16)
            act.dma_start(b2b[:], b2.partition_broadcast(P)).then_inc(ld_f, 16)
            for k, w in enumerate((wq, wk, wv, wo)):
                act.dma_start(wn[:, k], w).then_inc(ld_a, 16)
            act.dma_start(bob[:], bo.partition_broadcast(P)).then_inc(ld_a, 16)
            act.dma_start(bvb[:], bv.partition_broadcast(P)).then_inc(ld_a, 16)
            act.dma_start(rrep[:], r.partition_broadcast(HEADS)).then_inc(ld_a, 16)
            for stage, i in plan():
                if stage == "setup":
                    act.wait_ge(w2t_ps, 1)
                    act.activation(w2t[:].rearrange("p k o -> p (k o)"), bank[2][:], ACT.Copy, scale=0.5).then_inc(w2t_in, 1)
                if stage == "setup_att":
                    act.wait_ge(att_ps, 1)
                    act.activation(wah[:], bank[5][:], ACT.Copy).then_inc(wah_in, 1)
                    act.wait_ge(att_ps, 2)
                    act.activation(wvo[:].rearrange("p k o -> p (k o)"), bank[6][:, 0:2 * D], ACT.Copy).then_inc(wvo_in, 1)
                if stage == "turn":
                    act.wait_ge(s_xt, i + 1)
                    wait_xhl(act, i)
                    act.activation(xh[:, i % 2], ps_t[:], ACT.Copy).then_inc(s_hi, 1)
                if stage == "up":
                    for j in range(HB):
                        act.wait_ge(s_u, HB * i + j + 1)
                        if j == 0:
                            wait(act, s_d, i - 1)
                            if i == 0:
                                act.wait_ge(bcol_in, 1)
                        act.activation(gl[:, i % 2, j], ps_h[j % 2][:], ACT.Gelu, bias=bcol[:, j:j + 1]).then_inc(s_gelu, 1)
                if stage == "feat":
                    a, p = i
                    act.wait_ge(s_qk, NT * a + 2 * p + 2)
                    wait(act, s_red, 2 * a + p - 1)
                    act.activation(sq[:, p], halves(p, 0), ACT.Square, scale=0.25).then_inc(s_sq, 1)
                    act.wait_ge(s_sub, 2 * a + p + 1)
                    if p == 0:
                        wait(act, s_g, a - 1)
                        wait(act, s_qn, a - 1)
                    act.activation(qk[:, a % 2, 2 * p:2 * p + 2].rearrange("p n k d -> p (n k) d"), ex[:, p], ACT.Exp).then_inc(s_exp, 1)
                if stage == "qturn":
                    act.wait_ge(s_qt, i + 1)
                    wait(act, s_o, i - 3)
                    act.activation(qt[:, i % 4], ps_r[:], ACT.Copy).then_inc(s_qte, 1)
                if stage == "gram" and i % PER_B == PER_B - 1:
                    b = i // PER_B
                    act.wait_ge(s_g, i + 1)
                    wait(act, s_kvb, b)
                    act.activation(gs[:, 0:D + 1], ps_g[:, 0:D + 1], ACT.Copy).then_inc(s_gs, 1)

        @block.vector
        def _(dve):
            for stage, i in plan():
                if stage == "setup":
                    dve.wait_ge(w1t_ps, 1)
                    dve.tensor_copy(w1t[:], bank[1][:]).then_inc(w1t_in, 1)
                    dve.wait_ge(ld_f, 16 * 5)
                    dve.wait_ge(bcol_ps, 1)
                    dve.tensor_copy(bcol[:], bank[5][:, 0:HB + 4]).then_inc(bcol_in, 1)
                    dve.tensor_scalar(b2b[:], b2b[:], 0.5, None, ALU.mult).then_inc(scl_in, 1)
                    dve.tensor_copy(scl[:, 0:LORA], scb[:].to_broadcast([P, LORA])).then_inc(scl_in, 1)
                    dve.tensor_scalar(scl[:, LORA:], scb[:].to_broadcast([P, LORA]), 0.5, None, ALU.mult).then_inc(scl_in, 1)
                if stage == "setup_att":
                    dve.wait_ge(k_bd, 1)
                    dve.wait_ge(ld_a, 16 * 7)
                    dve.scalar_tensor_tensor(out=rbd[:].rearrange("p (h d) -> p h d", h=HEADS),
                                             in0=rrep[:].unsqueeze(1).to_broadcast([P, HEADS, HD]),
                                             scalar=float(HD) ** -0.5, in1=bd[:], op0=ALU.mult,
                                             op1=ALU.mult).then_inc(rbd_in, 1)
                    dve.wait_ge(wah_in, 1)
                    dve.tensor_tensor(wal[:], bank[5][:], wah[:].bitcast(F32), ALU.subtract).then_inc(wal_in, 1)
                    dve.wait_ge(att_ps, 3)
                    dve.tensor_copy(bhi[:], bank[7][0:2, :]).then_inc(bhi_in, 1)
                    dve.wait_ge(bhi_in, 1)
                    dve.wait_ge(k_neg, 1)
                    dve.wait_ge(k_brow, 1)
                    dve.scalar_tensor_tensor(out=brow[0:2, :], in0=bhi[:].bitcast(F32), scalar=negm[:, 0:1],
                                             in1=bank[7][0:2, :], op0=ALU.mult, op1=ALU.add).then_inc(brow_in, 1)
                if stage == "stats":
                    if i < CHUNKS:
                        dve.wait_ge(ld_x[i], 16)
                    else:
                        dve.wait_ge(s_x, i - CHUNKS + 1)
                    wait(dve, s_rstd, i - 1)
                    for n in range(NT):
                        ins = dve.bn_stats(bst[:, i % 2, n], X[:, i, n])
                    ins.then_inc(s_bst, 1)
                    dve.wait_ge(s_bst, i + 1)
                    wait(dve, s_xn, i - 1)
                    for n in range(NT):
                        ins = dve.bn_aggr(mv[:, i % 2, n], bst[:, i % 2, n])
                    ins.then_inc(s_mv, 1)
                    dve.wait_ge(s_mv, i + 1)
                    dve.tensor_scalar(veps[:, i % 2], mv[:, i % 2, :, 1], LN_EPS, None, ALU.add).then_inc(s_veps, 1)
                if stage == "norm":
                    dve.wait_ge(s_rstd, i + 1)
                    if i < CHUNKS or i >= 2 * CHUNKS:
                        wait(dve, s_xt, i - 1)
                        w = f_of(i) // PER_B
                        wait(dve, s_rows, 16 * w)
                    elif i >= CHUNKS + 4:
                        dve.wait_ge(s_g, i - 4 - CHUNKS + 1)
                    for n in range(NT):
                        ins = dve.tensor_scalar(xn[:, slot(i), n, 0:D], X[:, i, n], mv[:, i % 2, n, 0:1],
                                                rstd[:, i % 2, n:n + 1], ALU.subtract, ALU.mult)
                    ins.then_inc(s_xn, 1)
                if stage == "turn":
                    dve.wait_ge(s_hi, i + 1)
                    wait_xhl(dve, i)
                    dve.tensor_tensor(xl[:, i % 2], ps_t[:], xh[:, i % 2].bitcast(F32), ALU.subtract).then_inc(s_lo, 1)
                    if is_ffn(i) and i % PER_B == 0:
                        w = f_of(i) // PER_B
                        if w == 0:
                            dve.wait_ge(scl_in, 3)
                        wait(dve, s_w2m, w)
                        wait(dve, s_w1r, w)
                        dve.tensor_tensor(od[:], ps_t[:, 2:2 + 4 * LORA:2], scl[:], ALU.mult).then_inc(s_od, 1)
                if stage == "w1":
                    dve.wait_ge(s_ev, 16 * (i + 1))
                    dve.wait_ge(s_od, i + 1)
                    if i == 0:
                        dve.wait_ge(w1t_in, 1)
                    wait(dve, s_w1, i)
                    for j in range(LORA):
                        ins = dve.scalar_tensor_tensor(out=w1r[:, j], in0=ev[:, j], scalar=od[:, j:j + 1],
                                                       in1=w1t[:, j * D:(j + 1) * D], op0=ALU.mult, op1=ALU.add)
                    ins.then_inc(s_w1r, 1)
                    dve.wait_ge(s_w1r, i + 1)
                    wait(dve, s_u, HB * PER_B * i)
                    raw = w1r[:].rearrange("p i d -> p (i d)")
                    dve.tensor_copy(w1h[:], raw).then_inc(s_w1h, 1)
                    dve.wait_ge(s_w1h, i + 1)
                    dve.tensor_tensor(w1l[:], raw, w1h[:].bitcast(F32), ALU.subtract).then_inc(s_w1, 1)
                if stage == "down":
                    g = i if i < CHUNKS else i + CHUNKS
                    dve.wait_ge(s_d, i + 1)
                    add(dve, g, ps_y[i % 2])
                if stage == "feat":
                    a, p = i
                    dve.wait_ge(s_sq, 2 * a + p + 1)
                    dve.tensor_reduce(s8[:, p], sq[:, p].rearrange("p u (h d) -> p (u h) d", h=HEADS),
                                      AX.X, ALU.add).then_inc(s_red, 1)
                    dve.wait_ge(s_red, 2 * a + p + 1)
                    wait(dve, s_exp, 2 * a + p - 1)
                    dve.tensor_tensor(ex[:, p].rearrange("p u (h d) -> p u h d", h=HEADS),
                                      halves(p, 1).rearrange("p u (h d) -> p u h d", h=HEADS),
                                      s8[:, p].rearrange("p (u h) -> p u h", u=4).unsqueeze(3).to_broadcast([P, 4, HEADS, HD]),
                                      ALU.subtract).then_inc(s_sub, 1)
                if stage == "z":
                    dve.wait_ge(s_exp, 2 * i + 2)
                    dve.tensor_reduce(zs[:, 0], qk[:, i % 2, :, 0, :].rearrange("p n (h d) -> p n h d", h=HEADS),
                                      AX.X, ALU.add).then_inc(s_zs, 1)
                    dve.wait_ge(s_zs, i + 1)
                    dve.tensor_scalar(zs[:, 1], zs[:, 0], Z_EPS, None, ALU.add).then_inc(s_ze, 1)
                    dve.wait_ge(s_ze, i + 1)
                    wait(dve, s_qn, i)
                    dve.reciprocal(zr[:].rearrange("p n h -> p (n h)"), zs[:, 1]).then_inc(s_zr, 1)
                if stage == "mix":
                    b, k = i
                    if k == 0:
                        dve.wait_ge(s_gtp, b + 1)
                        dve.tensor_copy(gt[:], ps_m[:, 0:D]).then_inc(s_gt, 1)
                    if k == 1:
                        dve.wait_ge(s_kv, b + 1)
                        dve.scalar_tensor_tensor(out=kvb[:], in0=bvb[:], scalar=gs[:, D:D + 1], in1=ps_m[:, D:2 * D],
                                                 op0=ALU.mult, op1=ALU.add).then_inc(s_kvb, 1)
                        dve.wait_ge(s_kvb, b + 1)
                        dve.tensor_tensor(kvm[:], kvb[:], bd[:].rearrange("p h d -> p (h d)"), ALU.mult).then_inc(s_kvm, 1)
                    if k == 2:
                        dve.wait_ge(s_ktp, b + 1)
                        dve.tensor_copy(kvt[:], ps_m[:, 2 * D:3 * D]).then_inc(s_kt, 1)
                    if k == 3:
                        dve.wait_ge(s_mp, b + 1)
                        dve.tensor_copy(mo[:], ps_m[:, 3 * D:4 * D]).then_inc(s_mo, 1)
                if stage == "o":
                    b, k = i
                    a = PER_B * b + k
                    dve.wait_ge(s_o, a + 1)
                    add(dve, CHUNKS + a, ps_o[k])

        @block.tensor
        def _(pe):
            for stage, i in plan():
                if stage == "setup":
                    pe.wait_ge(k_id, 1)
                    pe.wait_ge(ld_w1, 16)
                    for j in range(HB):
                        ins = pe.transpose(bank[1][:, j * D:(j + 1) * D], w1n[:, j], ident[:])
                    ins.then_inc(w1t_ps, 1)
                    pe.wait_ge(ld_w2, 16)
                    for k in range(HB):
                        ins = pe.transpose(bank[2][:, k * D:(k + 1) * D], w2n[:, k * D:(k + 1) * D], ident[:])
                    ins.then_inc(w2t_ps, 1)
                    pe.wait_ge(ld_f, 16 * 5)
                    pe.transpose(bank[5][:, 0:HB + 4], brows[:], ident[0:HB + 4, 0:HB + 4]).then_inc(bcol_ps, 1)
                if stage == "setup_att":
                    pe.wait_ge(ld_a, 16 * 7)
                    pe.wait_ge(rbd_in, 1)
                    pe.wait_ge(bcol_in, 1)
                    for k in range(2):
                        pe.transpose(bank[5][:, 2 * k * D:(2 * k + 1) * D], wn[:, k], ident[:])
                        ins = pe.matmul(bank[5][:, (2 * k + 1) * D:(2 * k + 2) * D], wn[:, k], rbd[:], start=True, stop=True)
                    ins.then_inc(att_ps, 1)
                    for k in range(2):
                        ins = pe.transpose(bank[6][:, k * D:(k + 1) * D], wn[:, 2 + k], ident[:])
                    ins.then_inc(att_ps, 1)
                    for k in range(2):
                        pe.matmul(bank[7][0:2, 2 * k * D:(2 * k + 1) * D], bcol[:, HB + 2 * k:HB + 2 * k + 2], ident[:], start=True, stop=True)
                        ins = pe.matmul(bank[7][0:2, (2 * k + 1) * D:(2 * k + 2) * D], bcol[:, HB + 2 * k:HB + 2 * k + 2], rbd[:], start=True, stop=True)
                    ins.then_inc(att_ps, 1)
                if stage == "turn":
                    pe.wait_ge(s_xn, i + 1)
                    wait(pe, s_lo, i)
                    if i > 0:
                        before = i - 1
                        if is_ffn(before) and before % PER_B == 0:
                            pe.wait_ge(s_od, f_of(before) // PER_B + 1)
                    for n in range(NT):
                        ins = pe.transpose(ps_t[:, n * P:(n + 1) * P], xn[:, slot(i), n, 0:D], ident[:])
                    ins.then_inc(s_xt, 1)
                if stage == "up":
                    g = i if i < CHUNKS else i + CHUNKS
                    pe.wait_ge(s_lo, g + 1)
                    pe.wait_ge(s_w1, i // PER_B + 1)
                    if i == 0:
                        pe.wait_ge(w2t_in, 1)
                    if i == CHUNKS:
                        pe.wait_ge(s_sub, 2 * CHUNKS)
                    for j in range(HB):
                        wait(pe, s_gelu, HB * i + j - 1)
                        blk = slice(j * P, (j + 1) * P)
                        pe.matmul(ps_h[j % 2][:], w1h[:, blk], xh[:, g % 2], start=True, stop=False)
                        pe.matmul(ps_h[j % 2][:], w1h[:, blk], xl[:, g % 2], start=False, stop=False)
                        pe.matmul(ps_h[j % 2][:], w1l[:, blk], xh[:, g % 2], start=False, stop=True).then_inc(s_u, 1)
                if stage == "down":
                    g = i if i < CHUNKS else i + CHUNKS
                    pe.wait_ge(s_gelu, HB * (i + 1))
                    pe.wait_ge(s_w2, i // PER_B + 1)
                    wait(pe, s_x, g - 1)
                    for n in range(NT):
                        for j in range(HB):
                            ins = pe.matmul(ps_y[i % 2][:, n * P:(n + 1) * P], gl[:, i % 2, j, n * P:(n + 1) * P], w2e[:, j],
                                            start=(j == 0), stop=(j == HB - 1))
                    ins.then_inc(s_d, 1)
                if stage == "qk":
                    a, n = i
                    g = a + CHUNKS
                    if n == 0:
                        pe.wait_ge(s_lo, g + 1)
                        if a == 0:
                            pe.wait_ge(s_gelu, HB * CHUNKS)
                            pe.wait_ge(wal_in, 1)
                            pe.wait_ge(brow_in, 1)
                            pe.wait_ge(k_ones, 1)
                    if a == 0 and n >= 2:
                        pe.wait_ge(s_x, CHUNKS - 1 + n - 2)
                    if n % 2 == 0:
                        wait(pe, s_sub, 2 * a + n // 2 - 1)
                    to = quad[:, n, :]
                    tile = slice(n * P, (n + 1) * P)
                    pe.matmul(to, xh[:, g % 2, tile], wah[:], start=True, stop=False)
                    pe.matmul(to, xh[:, g % 2, tile], wal[:], start=False, stop=False)
                    pe.matmul(to, xl[:, g % 2, tile], wah[:], start=False, stop=False)
                    pe.matmul(to, ones[:], brow[:], start=False, stop=True).then_inc(s_qk, 1)
                if stage == "qturn":
                    pe.wait_ge(s_qn, i + 1)
                    if i == 0:
                        pe.wait_ge(wvo_in, 1)
                    wait(pe, s_qte, i)
                    if i % 2 == 1 and i >= 3:
                        pe.wait_ge(s_x, CHUNKS + i - 1)
                    for n in range(NT):
                        ins = pe.transpose(ps_r[:, n * P:(n + 1) * P], qn[:, n], ident[:])
                    ins.then_inc(s_qt, 1)
                if stage == "gram":
                    b, k = i // PER_B, i % PER_B
                    pe.wait_ge(s_exp, 2 * i + 2)
                    if i == 0:
                        pe.wait_ge(k_col, 1)
                    if k == 0:
                        wait(pe, s_gs, b)
                    for n in range(NT):
                        ins = pe.matmul(ps_g[:, 0:D + 1], qk[:, i % 2, n, 1, :], xn[:, slot(i + CHUNKS), n, 0:D + 1],
                                        start=(k == 0 and n == 0), stop=(k == PER_B - 1 and n == NT - 1))
                    ins.then_inc(s_g, 1)
                if stage == "mix":
                    b, k = i
                    if k == 0:
                        pe.wait_ge(s_gs, b + 1)
                        if b == 0:
                            pe.wait_ge(brow_in, 1)
                        if b > 0:
                            pe.wait_ge(s_x, CHUNKS + PER_B * (b - 1) + 1)
                        pe.transpose(ps_m[:, 0:D], gs[:, 0:D], ident[:]).then_inc(s_gtp, 1)
                    if k == 1:
                        pe.wait_ge(s_gt, b + 1)
                        pe.matmul(ps_m[:, D:2 * D], gt[:], wvo[:, 0], start=True, stop=True).then_inc(s_kv, 1)
                    if k == 2:
                        pe.wait_ge(s_kvm, b + 1)
                        pe.transpose(ps_m[:, 2 * D:3 * D], kvm[:], ident[:]).then_inc(s_ktp, 1)
                    if k == 3:
                        pe.wait_ge(s_kt, b + 1)
                        pe.matmul(ps_m[:, 3 * D:4 * D], kvt[:], wvo[:, 1], start=True, stop=True).then_inc(s_mp, 1)
                if stage == "o":
                    b, k = i
                    a = PER_B * b + k
                    pe.wait_ge(s_mo, b + 1)
                    pe.wait_ge(s_qte, a + 1)
                    if k == 1:
                        latest = min(a + 2, CHUNKS) if b < NB - 1 else CHUNKS
                        pe.wait_ge(s_qte, min(a + 2, CHUNKS))
                    for n in range(NT):
                        ins = pe.matmul(ps_o[k][:, n * P:(n + 1) * P], qt[:, a % 4, n * P:(n + 1) * P], mo[:],
                                        start=True, stop=True)
                    ins.then_inc(s_o, 1)


_INS = ['L0_attn_x', 'L0_attn_Wq', 'L0_attn_bq', 'L0_attn_Wk', 'L0_attn_bk', 'L0_attn_Wv', 'L0_attn_bv', 'L0_attn_Wo',
        'L0_attn_bo', 'L0_attn_R', 'L0_ffn_W1', 'L0_ffn_b1', 'L0_ffn_W2', 'L0_ffn_b2', 'L0_ffn_scale']


def kernel(**inputs):
    import numpy as _np
    import concourse.bacc as _bacc
    from concourse import mybir as _mybir
    from concourse.bass_utils import run_bass_kernel_spmd as _run

    nc = _bacc.Bacc("TRN2", target_bir_lowering=False, num_devices=1)
    arrays, args = {}, []
    for name in _INS:
        a = _np.ascontiguousarray(inputs[name])
        if a.ndim == 0:
            a = a.reshape(1)
        arrays[f"in_{name}_dram"] = a
        args.append(nc.dram_tensor(f"in_{name}_dram", a.shape, _mybir.dt.from_np(a.dtype), kind="ExternalInput").ap())
    args.append(nc.dram_tensor("out_0_dram", (NB, SEQ, D), _mybir.dt.float32, kind="ExternalOutput").ap())
    args.append(nc.dram_tensor("token_rows", (2 * NB, 4 * LORA, D), _mybir.dt.float32, kind="Internal").ap())
    build(nc, *args)
    r = _run(nc, [arrays], core_ids=[0])
    return r.results[0]["out_0_dram"]
```

```python
import numpy as np
from contextlib import ExitStack

import concourse.bass as bass
from concourse import mybir

ALU = mybir.AluOpType
ACT = mybir.ActivationFunctionType
AX = mybir.AxisListType
F32 = mybir.dt.float32
F32R = mybir.dt.float32r

P = 128
D = 128
H = 512
NB, SEQ = 4, 1024
HEADS, HD = 16, 8
TOK = 512
NT = TOK // P
CHUNKS = NB * SEQ // TOK
PER_B = SEQ // TOK
HB = H // P
LORA = 4
LN_EPS, Z_EPS = 1e-5, 1e-8
WARM_UP = (11, 4)
SHIFT = 0.125
FC = 2 * CHUNKS


TIMES = {
    "sp": (
        {
            "rows": (44.802, None),
        },
        {
        },
        {
            "rows": (52.056, None), "down 3": (71.517, 71.608),
        },
    ),
    "pool": (
        {
            "stats": (-6.35, -6.106), "w2": (-4.658, None), "norm": (-3.167, -3.95), "astats": (-1.196, -1.965),
            "anorm": (25.035, 25.166),
        },
        {
            "z": (16.076, 17.062),
        },
        {
            "stats": (13.032, 13.372), "w2": (14.486, None), "norm": (15.157, 14.724),
        },
    ),
    "act": (
        {
            "load": (-0.978, None), "turn": (-0.252, -0.671), "up 0": (0.354, 0.305), "up 1": (0.52, 0.547),
            "up 2": (0.924, 0.634), "up 3": (0.928, 0.734), "anorm": (3.471, 2.837), "aturn": (6.088, 6.67),
            "split weights": (7.092, None),
        },
        {
            "feat 0": (1.754, 1.191), "feat 1": (1.861, 1.957), "exp 0": (1.955, 2.446), "exp 1": (2.571, 2.701),
            "gram": (None, 3.353), "qturn": (6.132, 5.752),
        },
        {
            "turn": (2.206, 2.703), "up 0": (3.166, 2.841), "up 1": (3.542, 3.009), "up 2": (3.766, 3.03),
            "up 3": (3.804, 3.498),
        },
    ),
    "dve": (
        {
            "stats": (-5.611, -5.514), "scale": (-4.956, None), "norm": (-4.175, -4.52), "turn": (-3.037, -3.767),
            "odd": (-3.387, None), "w1": (-2.864, None), "constants": (-2.061, None), "down 3": (-0.747, -1.217),
            "astats": (-0.698, -0.871), "anorm": (-0.219, 0.094), "aturn": (3.545, 3.521),
            "split weights": (4.059, None),
        },
        {
            "feat 0": (-1.374, -1.356), "feat 1": (-1.189, -0.755), "z": (0.615, 0.406), "mix 0": (None, 1.619),
            "mix 1": (None, 1.791), "mix 2": (None, 2.094), "mix 3": (None, 2.562), "o": (4.217, 3.787),
        },
        {
            "stats": (-2.317, -2.035), "norm": (-1.416, -1.395), "turn": (-0.902, -0.693), "odd": (-0.899, None),
            "w1": (-0.414, None), "down 3": (2.305, 1.478),
        },
    ),
    "pe": (
        {
            "warm up 0": (-29.552, None), "warm up 1": (-1.094, None), "turn": (-0.44, -0.68),
            "up 0": (0.497, 0.057), "up 1": (0.539, 0.118), "up 2": (0.765, 0.74), "up 3": (0.802, 0.743),
            "down 0": (1.418, 1.053), "down 1": (1.451, 1.124), "down 2": (1.755, 1.638), "down 3": (1.913, 1.822),
            "split weights": (2.344, None), "aturn": (6.467, 6.239),
        },
        {
            "qk 0": (1.766, 1.663), "qk 1": (1.994, 1.98), "qk 2": (2.039, 2.034), "qk 3": (2.342, 2.075),
            "gram": (4.388, 3.594), "mix 0": (None, 5.264), "qturn": (5.428, 5.982), "mix 1": (None, 5.451),
            "mix 2": (None, 5.887), "mix 3": (None, 5.995), "o": (7.306, 6.846),
        },
        {
            "turn": (2.651, 2.507), "up 0": (3.431, 2.962), "up 1": (3.449, 2.99), "up 2": (3.572, 3.357),
            "up 3": (3.611, 3.552), "down 0": (4.017, 3.962), "down 1": (4.067, 4.304), "down 2": (4.804, 4.407),
            "down 3": (4.916, 4.671),
        },
    ),
}
APART = {
    ("dve", "stats", 2): -4.608,
    ("dve", "feat", (3, 0)): -1.351,
    ("dve", "z", 4): 0.61,
    ("dve", "z", 7): 1.625,
    ("dve", "o", 5): 3.35,
    ("dve", "stats", 10): -1.654,
    ("act", "up", (5, 2)): 0.629,
    ("act", "anorm", 7): 5.188,
}


def work():
    for stage in ("load", "scale", "constants", "split weights"):
        yield stage, 0, 0, 0
    for k in range(2):
        yield "warm up", (0, k), 0, 0
    for k in range(2):
        yield "warm up", k, 0, 0
    for f in range(FC):
        phase, step = (0, f) if f < CHUNKS else (2, f + CHUNKS)
        for stage in ("stats", "norm", "turn"):
            yield stage, f, phase, step
        if f % PER_B == 0:
            for stage in ("rows", "odd", "w1", "w2"):
                yield stage, f // PER_B, phase, step
        for j in range(HB):
            yield "up", (f, j), phase, step
        for n in range(NT):
            yield "down", (f, n), phase, step
    for a in range(CHUNKS):
        for stage in ("astats", "anorm", "aturn"):
            yield stage, a, 0, a
        for n in range(NT):
            yield "qk", (a, n), 1, CHUNKS + a
        for p in range(2):
            yield "feat", (a, p), 1, CHUNKS + a
            yield "exp", (a, p), 1, CHUNKS + a
        for stage in ("z", "gram", "qturn", "o"):
            yield stage, a, 1, CHUNKS + a
        if a % PER_B == PER_B - 1:
            for k in range(4):
                yield "mix", (a // PER_B, k), 1, CHUNKS + a


def plan(engine):
    placed = []
    for stage, i, phase, step in work():
        name = f"{stage} {i[1]}" if isinstance(i, tuple) else stage
        time = TIMES[engine][phase].get(name, (None, None))[step % 2]
        if time is not None:
            placed.append((step + APART.get((engine, stage, i), time), stage, i))
    placed.sort(key=lambda p: p[0])
    return [(stage, i) for _, stage, i in placed]


def stats(dve, i, x, bst, mv, veps, s_bst, s_mv, s_veps, s_rstd, s_xn):
    if i >= 2:
        dve.wait_ge(s_rstd, i - 1)
        dve.wait_ge(s_xn, NT * (i - 1))
    for n in range(NT):
        ins = dve.bn_stats(bst[:, i % 2, n], x[:, n])
    ins.then_inc(s_bst, 1)
    dve.wait_ge(s_bst, i + 1)
    for n in range(NT):
        ins = dve.bn_aggr(mv[:, i % 2, n], bst[:, i % 2, n])
    ins.then_inc(s_mv, 1)
    dve.wait_ge(s_mv, i + 1)
    dve.tensor_scalar(veps[:, i % 2], mv[:, i % 2, :, 1], LN_EPS, None, ALU.add).then_inc(s_veps, 1)


def build(nc, x, w1t_in, w2t_in, wa_in, cols_in, rows_in, r_in, out, token_rows):
    ctx = ExitStack()
    with ctx:
        def sb(name, shape, dt=F32):
            return ctx.enter_context(nc.sbuf_tensor(name, shape, dt))

        def sem(name):
            return ctx.enter_context(nc.semaphore(name))

        X = sb("X", [P, 3 * CHUNKS, NT, D])
        bst = sb("bst", [P, 2, NT, 6])
        mv = sb("mv", [P, 2, NT, 2])
        veps = sb("veps", [P, 2, NT])
        rstd = sb("rstd", [P, 2, NT])
        mhalf = sb("mhalf", [P, NT])
        table = sb("table", [P, 1])
        xn = sb("xn", [P, 2, NT, D])
        xh = sb("xh", [P, 2, TOK], F32R)
        xl = sb("xl", [P, 2, TOK], F32R)
        abst = sb("abst", [P, 2, NT, 6])
        amv = sb("amv", [P, 2, NT, 2])
        aveps = sb("aveps", [P, 2, NT])
        arstd = sb("arstd", [P, 2, NT])
        amr = sb("amr", [P, 2, NT])
        anmr = sb("anmr", [P, 2, NT])
        xa = sb("xa", [P, CHUNKS, NT, D])
        xah = sb("xah", [P, CHUNKS, TOK], F32R)
        xal = sb("xal", [P, CHUNKS, TOK], F32R)
        gl = sb("gl", [P, 2, HB, TOK])
        w1t = sb("w1t", [P, H])
        w2n = sb("w2n", [P, HB, D])
        w2t = sb("w2t", [P, HB, D])
        ev = sb("ev", [P, 2 * LORA, D])
        od = sb("od", [P, 2 * LORA])
        scl = sb("scl", [P, 2 * LORA])
        w1r = sb("w1r", [P, LORA, D])
        w1h = sb("w1h", [P, 2, H], F32R)
        w1l = sb("w1l", [P, 2, H], F32R)
        w2m = sb("w2m", [P, LORA, D])
        w2e = sb("w2e", [P, 2, HB, D])
        cols = sb("cols", [P, HB + 3])
        rows = sb("rows", [P, 2 * D + 1])
        b2h = sb("b2h", [P, D])
        ident = sb("ident", [P, P])
        bd = sb("bd", [P, HEADS, HD])
        rrep = sb("rrep", [P, HD])
        irbd = sb("irbd", [P, 2, P])
        wa = sb("wa", [P, 4, D])
        wsum = sb("wsum", [P, 3])
        vd = sb("vd", [P, 3])
        vs = sb("vs", [P, 3])
        wb = sb("wb", [P, 3, D])
        wv2 = sb("wv2", [P, D])
        wah = sb("wah", [P, TOK], F32R)
        wal = sb("wal", [P, TOK], F32R)
        sq = sb("sq", [P, 2, 4, P])
        s8 = sb("s8", [P, 2, 4 * HEADS])
        ex = sb("ex", [P, 2, 4, P])
        qk = sb("qk", [P, 2, NT, 2, P])
        zs = sb("zs", [P, 2, NT * HEADS])
        zr = sb("zr", [P, NT, HEADS])
        qn = sb("qn", [P, 2, NT, P])
        qt = sb("qt", [P, 4, TOK])
        gs = sb("gs", [P, D])
        gt = sb("gt", [P, D])
        kvm = sb("kvm", [P, D])
        kvt = sb("kvt", [P, D])
        mo = sb("mo", [P, D])

        def bank(name):
            return ctx.enter_context(nc.psum_tensor(name, [P, TOK], F32))

        ps_t = bank("ps_t")
        quad = ctx.enter_context(nc.psum_tensor("quad", [P, NT, TOK], F32))
        ps_h = [quad[:, 0], quad[:, 1]]
        ps_y = [quad[:, 2], quad[:, 3]]
        ps_g, ps_r, ps_m = bank("ps_g"), bank("ps_r"), bank("ps_m")
        ps_o = [ps_t] * (CHUNKS - 4) + [ps_m] * 3 + [ps_r]

        ld_x = [sem(f"ld_x{c}") for c in range(CHUNKS)]
        ld_w1, ld_w2, ld_cols, ld_rows, ld_wa, ld_r = [sem(f"ld_{n}") for n in ("w1", "w2", "cols", "rows", "wa", "r")]
        k_exp, k_sel, k_zero, k_id, k_bd0, k_bd1, k_bd = [sem(f"k_{n}") for n in ("exp", "sel", "zero", "id", "bd0", "bd1", "bd")]
        k_scl, k_b2h, k_w2t, k_rbd, k_wsum, k_vd = [sem(f"k_{n}") for n in ("scl", "b2h", "w2t", "rbd", "wsum", "vd")]
        k_vs, k_wb, k_war, k_wv, k_wah, k_wal, k_wv2 = [sem(f"k_{n}") for n in ("vs", "wb", "war", "wv", "wah", "wal", "wv2")]
        s_bst, s_mv, s_veps, s_rstd, s_xn, s_xt, s_hi, s_lo, s_xb = [
            sem(f"s_{n}") for n in ("bst", "mv", "veps", "rstd", "xn", "xt", "hi", "lo", "xb")]
        s_u, s_gelu, s_d = sem("s_u"), sem("s_gelu"), sem("s_d")
        s_x1, s_x3 = sem("s_x1"), sem("s_x3")
        s_rows, s_ev = sem("s_rows"), sem("s_ev")
        s_od, s_w1r, s_w1h, s_w1, s_w2m, s_w2 = [sem(f"s_{n}") for n in ("od", "w1r", "w1h", "w1", "w2m", "w2")]
        a_bst, a_mv, a_veps, a_rstd, a_mr, a_nmr, a_xn, a_xt, a_hi, a_lo, a_xb = [
            sem(f"a_{n}") for n in ("bst", "mv", "veps", "rstd", "mr", "nmr", "xn", "xt", "hi", "lo", "xb")]
        s_qk = sem("s_qk")
        s_sq, s_red, s_sub, s_exp = [sem(f"s_{n}") for n in ("sq", "red", "sub", "exp")]
        s_zs, s_ze, s_zr, s_qn, s_qt, s_qte, s_g, s_o, s_x2 = [
            sem(f"s_{n}") for n in ("zs", "ze", "zr", "qn", "qt", "qte", "g", "o", "x2")]
        m_gs, m_gtp, m_gt, m_kv, m_kvm, m_ktp, m_kt, m_mp, m_mo = [
            sem(f"m_{n}") for n in ("gs", "gtp", "gt", "kv", "kvm", "ktp", "kt", "mp", "mo")]
        s_out = sem("s_out")

        def chunk_of(t, c):
            flat = t.rearrange("b s d -> (b s) d")
            return flat[c * TOK:(c + 1) * TOK, :].rearrange("(n p) d -> p n d", p=P)

        def wait(eng, s, n):
            if n > 0:
                eng.wait_ge(s, n)

        def xslot(f):
            return f if f < CHUNKS else f + CHUNKS

        def halves(p, which):
            return quad[:, 2 * p:2 * p + 2, :].rearrange("p n (k w d) -> p w (n k) d", k=2, w=2)[:, which]

        def flat(t):
            return t.rearrange("p n d -> p (n d)")

        def heads(t):
            return t.rearrange("p n (h d) -> p n h d", h=HEADS)

        block = ctx.enter_context(nc.Block())

        @block.sync
        def _(sp):
            sp.dma_start(X[:, 0], chunk_of(x, 0)).then_inc(ld_x[0], 16)
            sp.dma_start(rows[:], rows_in.partition_broadcast(P)).then_inc(ld_rows, 16)
            sp.dma_start(w1t[:], w1t_in).then_inc(ld_w1, 16)
            sp.dma_start(X[:, 1], chunk_of(x, 1)).then_inc(ld_x[1], 16)
            sp.dma_start(cols[:], cols_in).then_inc(ld_cols, 16)
            sp.dma_start(w2n[:], w2t_in).then_inc(ld_w2, 16)
            sp.dma_start(X[:, 2], chunk_of(x, 2)).then_inc(ld_x[2], 16)
            sp.dma_start(wa[:], wa_in).then_inc(ld_wa, 16)
            sp.dma_start(rrep[:], r_in.partition_broadcast(HEADS)).then_inc(ld_r, 16)
            for stage, i in plan("sp"):
                if stage == "rows":
                    sp.wait_ge(s_xn, NT * PER_B * i + 1)
                    sp.dma_start(token_rows[i], xn[1:1 + 4 * LORA, 0, 0, :]).then_inc(s_rows, 16)
                    sp.wait_ge(s_rows, 16 * (i + 1))
                    wait(sp, s_w1r, LORA * i)
                    wait(sp, s_w2m, i)
                    even = token_rows[i].rearrange("(n two) d -> two n d", two=2)[0]
                    sp.dma_start(ev[:], even.partition_broadcast(P)).then_inc(s_ev, 16)
                    if i == 0:
                        for c in range(3, CHUNKS):
                            sp.dma_start(X[:, c], chunk_of(x, c)).then_inc(ld_x[c], 16)
                if stage == "down" and i[0] >= CHUNKS and i[1] == NT - 1:
                    c = i[0] - CHUNKS
                    parts = 2 if c == CHUNKS - 1 else 1
                    for h in range(parts):
                        tiles = slice(NT // parts * h, NT // parts * (h + 1))
                        sp.wait_ge(s_x3, c + h + 1)
                        sp.dma_start(chunk_of(out, c)[:, tiles], X[:, xslot(i[0]), tiles]).then_inc(s_out, 16)
            sp.wait_ge(s_out, 16 * (CHUNKS + 1))

        @block.gpsimd
        def _(pool):
            pool.memset(mhalf[:], -0.5).then_inc(k_exp, 1)
            pool.memset(ident[:], 0.0).then_inc(k_zero, 1)
            pool.wait_ge(k_zero, 1)
            pool.affine_select(out=ident[:], in_=ident[:], compare_op=ALU.not_equal, fill=1.0, base=0,
                               pattern=[[-1, P]], channel_multiplier=1).then_inc(k_id, 1)
            pool.memset(irbd[:, 0], 0.0).then_inc(k_zero, 1)
            pool.wait_ge(k_zero, 2)
            pool.affine_select(out=irbd[:, 0], in_=irbd[:, 0], compare_op=ALU.not_equal, fill=1.0, base=0,
                               pattern=[[-1, P]], channel_multiplier=1).then_inc(k_id, 1)
            pool.memset(bd[:], 1.0).then_inc(k_bd0, 1)
            pool.wait_ge(k_bd0, 1)
            pool.affine_select(out=bd[:], in_=bd[:], compare_op=ALU.is_ge, fill=0.0, base=0,
                               pattern=[[-HD, HEADS], [0, HD]], channel_multiplier=1).then_inc(k_bd1, 1)
            pool.wait_ge(k_bd1, 1)
            pool.affine_select(out=bd[:], in_=bd[:], compare_op=ALU.is_ge, fill=0.0, base=HD - 1,
                               pattern=[[HD, HEADS], [0, HD]], channel_multiplier=-1).then_inc(k_bd, 1)
            for stage, i in plan("pool"):
                if stage == "stats":
                    pool.wait_ge(s_veps, i + 1)
                    if i == 0:
                        pool.wait_ge(k_exp, 1)
                    wait(pool, s_xn, NT * (i - 1))
                    pool.tensor_tensor(rstd[:, i % 2], veps[:, i % 2], mhalf[:], ALU.pow).then_inc(s_rstd, 1)
                if stage == "astats":
                    pool.wait_ge(a_veps, i + 1)
                    wait(pool, a_xn, NT * (i - 1))
                    pool.tensor_tensor(arstd[:, i % 2], aveps[:, i % 2], mhalf[:], ALU.pow).then_inc(a_rstd, 1)
                if stage == "norm":
                    pool.wait_ge(s_xn, NT * (i + 1))
                    if i == 0:
                        pool.wait_ge(k_b2h, 1)
                    pool.tensor_tensor(X[:, xslot(i)], X[:, xslot(i)], b2h[:].unsqueeze(1).to_broadcast([P, NT, D]),
                                       ALU.add).then_inc(s_xb, 1)
                if stage == "anorm":
                    pool.wait_ge(a_xn, NT * (i + 1))
                    pool.tensor_tensor(X[:, CHUNKS + i], X[:, CHUNKS + i],
                                       rows[:, D:2 * D].unsqueeze(1).to_broadcast([P, NT, D]), ALU.add).then_inc(a_xb, 1)
                if stage == "w2":
                    pool.wait_ge(s_ev, 16 * (i + 1))
                    pool.wait_ge(s_od, i + 1)
                    wait(pool, s_w2, i)
                    pool.tensor_tensor(w2m[:], ev[:, LORA:2 * LORA],
                                       od[:, LORA:2 * LORA].unsqueeze(2).to_broadcast([P, LORA, D]),
                                       ALU.mult).then_inc(s_w2m, 1)
                    pool.wait_ge(s_w2m, i + 1)
                    if i == 0:
                        pool.wait_ge(k_w2t, 1)
                    wait(pool, s_d, NT * PER_B * (i - 1))
                    pool.tensor_tensor(w2e[:, i % 2], flat(w2m[:]).rearrange("p (o k) -> p k o", k=HB),
                                       w2t[:], ALU.add).then_inc(s_w2, 1)
                if stage == "z":
                    pool.wait_ge(s_zr, i + 1)
                    wait(pool, s_qt, i - 1)
                    pool.tensor_tensor(heads(qn[:, i % 2]), heads(qk[:, i % 2, :, 0, :]),
                                       zr[:].unsqueeze(3).to_broadcast([P, NT, HEADS, HD]),
                                       ALU.mult).then_inc(s_qn, 1)

        @block.scalar
        def _(act):
            act.wait_ge(k_exp, 1)
            act.activation(table[:], mhalf[:, 0:1], ACT.Gelu)
            for stage, i in plan("act"):
                if stage == "load":
                    act.wait_ge(ld_w2, 16)
                    act.activation(flat(w2t[:]), flat(w2n[:]), ACT.Copy, scale=0.5).then_inc(k_w2t, 1)
                if stage == "split weights":
                    act.wait_ge(k_war, 1)
                    act.activation(wah[:], ps_r[:], ACT.Copy).then_inc(k_wah, 1)
                if stage == "turn":
                    act.wait_ge(s_xt, i + 1)
                    wait(act, s_u, HB * (i - 1))
                    act.activation(xh[:, i % 2], ps_t[:], ACT.Copy).then_inc(s_hi, 1)
                if stage == "aturn":
                    act.wait_ge(a_xt, i + 1)
                    act.activation(xah[:, i], ps_m[:], ACT.Copy).then_inc(a_hi, 1)
                if stage == "anorm":
                    act.wait_ge(a_nmr, i + 1)
                    for n in range(NT):
                        act.activation(xa[:, i, n], X[:, CHUNKS + i, n], ACT.Identity, bias=anmr[:, i % 2, n:n + 1],
                                       scale=arstd[:, i % 2, n:n + 1]).then_inc(a_xn, 1)
                if stage == "up":
                    f, j = i
                    act.wait_ge(s_u, HB * f + j + 1)
                    if j == 0:
                        wait(act, s_d, NT * (f - 1))
                        if f == 0:
                            act.wait_ge(ld_cols, 16)
                    act.activation(gl[:, f % 2, j], ps_h[j % 2], ACT.Gelu, bias=cols[:, j:j + 1]).then_inc(s_gelu, 1)
                if stage == "feat":
                    a, p = i
                    act.wait_ge(s_qk, NT * a + 2 * p + 2)
                    wait(act, s_red, 2 * a + p - 1)
                    act.activation(sq[:, p], halves(p, 0), ACT.Square, scale=0.25).then_inc(s_sq, 1)
                if stage == "exp":
                    a, p = i
                    act.wait_ge(s_sub, 2 * a + p + 1)
                    if p == 0:
                        wait(act, s_g, a - 1)
                        wait(act, s_qn, a - 1)
                    act.activation(qk[:, a % 2, 2 * p:2 * p + 2].rearrange("p n k d -> p (n k) d"), ex[:, p],
                                   ACT.Exp).then_inc(s_exp, 1)
                if stage == "qturn":
                    act.wait_ge(s_qt, i + 1)
                    wait(act, s_o, i - 3)
                    act.activation(qt[:, i % 4], ps_r[:], ACT.Copy).then_inc(s_qte, 1)
                if stage == "gram" and i % PER_B == PER_B - 1:
                    b = i // PER_B
                    act.wait_ge(s_g, i + 1)
                    wait(act, m_gtp, b)
                    act.activation(gs[:], ps_g[:, 0:D], ACT.Copy).then_inc(m_gs, 1)

        @block.vector
        def _(dve):
            for stage, i in plan("dve"):
                if stage == "constants":
                    dve.wait_ge(k_bd, 1)
                    dve.wait_ge(ld_r, 16)
                    dve.scalar_tensor_tensor(out=irbd[:, 1].rearrange("p (h d) -> p h d", h=HEADS),
                                             in0=rrep[:].unsqueeze(1).to_broadcast([P, HEADS, HD]),
                                             scalar=float(HD) ** -0.5, in1=bd[:], op0=ALU.mult,
                                             op1=ALU.mult).then_inc(k_rbd, 1)
                    dve.wait_ge(ld_wa, 16)
                    dve.tensor_reduce(wsum[:], wa[:, 0:3], AX.X, ALU.add).then_inc(k_wsum, 1)
                    dve.wait_ge(k_wsum, 1)
                    dve.wait_ge(ld_cols, 16)
                    dve.scalar_tensor_tensor(out=vd[:], in0=wsum[:], scalar=-SHIFT, in1=cols[:, HB:HB + 3],
                                             op0=ALU.mult, op1=ALU.add).then_inc(k_vd, 1)
                    dve.wait_ge(k_vd, 1)
                    dve.tensor_scalar(vs[:], vd[:], 1.0 / (D * SHIFT), None, ALU.mult).then_inc(k_vs, 1)
                    dve.wait_ge(k_vs, 1)
                    for k in range(3):
                        ins = dve.tensor_scalar(wb[:, k], wa[:, k], vs[:, k:k + 1], None, ALU.add)
                    ins.then_inc(k_wb, 1)
                if stage == "split weights":
                    dve.wait_ge(k_wah, 1)
                    dve.tensor_tensor(wal[:], ps_r[:], wah[:].bitcast(F32), ALU.subtract).then_inc(k_wal, 1)
                    dve.wait_ge(k_wv, 1)
                    dve.tensor_copy(wv2[:], ps_g[:, 0:D]).then_inc(k_wv2, 1)
                if stage == "stats":
                    if i < CHUNKS:
                        dve.wait_ge(ld_x[i], 16)
                    else:
                        dve.wait_ge(s_x2, i - CHUNKS + 1)
                    stats(dve, i, X[:, xslot(i)], bst, mv, veps, s_bst, s_mv, s_veps, s_rstd, s_xn)
                if stage == "norm":
                    dve.wait_ge(s_rstd, i + 1)
                    wait(dve, s_xt, i - 1)
                    wait(dve, s_rows, 16 * (i // PER_B))
                    for n in range(NT):
                        dve.tensor_scalar(xn[:, i % 2, n], X[:, xslot(i), n], mv[:, i % 2, n, 0:1],
                                          rstd[:, i % 2, n:n + 1], ALU.subtract, ALU.mult).then_inc(s_xn, 1)
                if stage == "scale":
                    dve.wait_ge(ld_rows, 16)
                    dve.tensor_scalar(b2h[:], rows[:, 0:D], 0.5, None, ALU.mult).then_inc(k_b2h, 1)
                    s = rows[:, 2 * D:2 * D + 1].to_broadcast([P, LORA])
                    dve.tensor_copy(scl[:, 0:LORA], s).then_inc(k_scl, 1)
                    dve.tensor_scalar(scl[:, LORA:], s, 0.5, None, ALU.mult).then_inc(k_scl, 1)
                if stage == "astats":
                    dve.wait_ge(s_x1, i + 1)
                    stats(dve, i, X[:, CHUNKS + i], abst, amv, aveps, a_bst, a_mv, a_veps, a_rstd, a_xn)
                if stage == "anorm":
                    dve.wait_ge(a_rstd, i + 1)
                    wait(dve, a_xn, NT * (i - 1))
                    dve.tensor_tensor(amr[:, i % 2], amv[:, i % 2, :, 0], arstd[:, i % 2], ALU.mult).then_inc(a_mr, 1)
                    dve.wait_ge(a_mr, i + 1)
                    dve.tensor_scalar(anmr[:, i % 2], amr[:, i % 2], -1.0, SHIFT, ALU.mult, ALU.add).then_inc(a_nmr, 1)
                if stage == "turn":
                    dve.wait_ge(s_hi, i + 1)
                    wait(dve, s_u, HB * (i - 1))
                    dve.tensor_tensor(xl[:, i % 2], ps_t[:], xh[:, i % 2].bitcast(F32), ALU.subtract).then_inc(s_lo, 1)
                if stage == "odd":
                    dve.wait_ge(s_hi, PER_B * i + 1)
                    if i == 0:
                        dve.wait_ge(k_scl, 2)
                    wait(dve, s_w2m, i)
                    wait(dve, s_w1r, LORA * i)
                    dve.tensor_tensor(od[:], ps_t[:, 2:2 + 4 * LORA:2], scl[:], ALU.mult).then_inc(s_od, 1)
                if stage == "aturn":
                    dve.wait_ge(a_hi, i + 1)
                    dve.tensor_tensor(xal[:, i], ps_m[:], xah[:, i].bitcast(F32), ALU.subtract).then_inc(a_lo, 1)
                if stage == "w1":
                    dve.wait_ge(s_od, i + 1)
                    if i == 0:
                        dve.wait_ge(ld_w1, 16)
                        dve.wait_ge(k_sel, 1)
                    else:
                        dve.wait_ge(s_ev, 16 * (i + 1))
                        dve.wait_ge(s_w1, LORA * i)
                    even = ps_m[:].rearrange("p (j d) -> p j d", j=LORA) if i == 0 else ev
                    for j in range(LORA + 2):
                        if j < LORA:
                            dve.scalar_tensor_tensor(out=w1r[:, j], in0=even[:, j], scalar=od[:, j:j + 1],
                                                     in1=w1t[:, j * D:(j + 1) * D], op0=ALU.mult,
                                                     op1=ALU.add).then_inc(s_w1r, 1)
                        if 1 <= j <= LORA:
                            dve.wait_ge(s_w1r, LORA * i + j)
                            if j == 1:
                                wait(dve, s_u, HB * PER_B * (i - 1))
                            dve.tensor_copy(w1h[:, i % 2, (j - 1) * D:j * D], w1r[:, j - 1]).then_inc(s_w1h, 1)
                        if j >= 2:
                            blk = slice((j - 2) * D, (j - 1) * D)
                            dve.wait_ge(s_w1h, LORA * i + j - 1)
                            dve.tensor_tensor(w1l[:, i % 2, blk], w1r[:, j - 2], w1h[:, i % 2, blk].bitcast(F32),
                                              ALU.subtract).then_inc(s_w1, 1)
                if stage == "down" and i[1] == NT - 1:
                    f = i[0]
                    to = CHUNKS + f if f < CHUNKS else xslot(f)
                    dve.wait_ge(s_xb, f + 1)
                    parts = 2 if f == FC - 1 else 1
                    for h in range(parts):
                        tiles, part = NT // parts, TOK // parts
                        dve.wait_ge(s_d, NT * f + tiles * (h + 1))
                        dve.tensor_tensor(flat(X[:, to, tiles * h:tiles * (h + 1)]),
                                          (ps_g if h == 1 else ps_y[f % 2])[:, part * h:part * (h + 1)],
                                          flat(X[:, xslot(f), tiles * h:tiles * (h + 1)]), ALU.add).then_inc(
                            s_x1 if f < CHUNKS else s_x3, 1)
                if stage == "feat":
                    a, p = i
                    dve.wait_ge(s_sq, 2 * a + p + 1)
                    dve.tensor_reduce(s8[:, p], sq[:, p].rearrange("p u (h d) -> p (u h) d", h=HEADS),
                                      AX.X, ALU.add).then_inc(s_red, 1)
                    dve.wait_ge(s_red, 2 * a + p + 1)
                    wait(dve, s_exp, 2 * a + p - 1)
                    dve.tensor_tensor(heads(ex[:, p]), heads(halves(p, 1)),
                                      s8[:, p].rearrange("p (u h) -> p u h", u=4).unsqueeze(3).to_broadcast([P, 4, HEADS, HD]),
                                      ALU.subtract).then_inc(s_sub, 1)
                if stage == "z":
                    dve.wait_ge(s_exp, 2 * i + 2)
                    dve.tensor_reduce(zs[:, 0], heads(qk[:, i % 2, :, 0, :]), AX.X, ALU.add).then_inc(s_zs, 1)
                    dve.wait_ge(s_zs, i + 1)
                    dve.tensor_scalar(zs[:, 1], zs[:, 0], Z_EPS, None, ALU.add).then_inc(s_ze, 1)
                    dve.wait_ge(s_ze, i + 1)
                    wait(dve, s_qn, i)
                    dve.reciprocal(flat(zr[:]), zs[:, 1]).then_inc(s_zr, 1)
                if stage == "mix":
                    b, k = i
                    if k == 0:
                        dve.wait_ge(m_gtp, b + 1)
                        dve.tensor_copy(gt[:], ps_m[:, 0:D]).then_inc(m_gt, 1)
                    if k == 1:
                        dve.wait_ge(m_kv, b + 1)
                        dve.tensor_tensor(kvm[:], ps_m[:, D:2 * D], flat(bd[:]), ALU.mult).then_inc(m_kvm, 1)
                    if k == 2:
                        dve.wait_ge(m_ktp, b + 1)
                        dve.tensor_copy(kvt[:], ps_m[:, 2 * D:3 * D]).then_inc(m_kt, 1)
                    if k == 3:
                        dve.wait_ge(m_mp, b + 1)
                        wait(dve, s_o, PER_B * b)
                        dve.tensor_copy(mo[:], ps_m[:, 3 * D:4 * D]).then_inc(m_mo, 1)
                if stage == "o":
                    dve.wait_ge(s_o, i + 1)
                    dve.wait_ge(a_xb, i + 1)
                    dve.tensor_tensor(flat(X[:, 2 * CHUNKS + i]), ps_o[i][:], flat(X[:, CHUNKS + i]),
                                      ALU.add).then_inc(s_x2, 1)

        @block.tensor
        def _(pe):
            for stage, i in plan("pe"):
                if stage == "split weights":
                    pe.wait_ge(k_wb, 1)
                    pe.wait_ge(k_id, 2)
                    pe.wait_ge(k_rbd, 1)
                    for k in range(2):
                        ins = pe.matmul(ps_r[:, 2 * k * D:2 * (k + 1) * D], wb[:, k], flat(irbd[:]), start=True, stop=True)
                    ins.then_inc(k_war, 1)
                    pe.transpose(ps_g[:, 0:D], wb[:, 2], ident[:]).then_inc(k_wv, 1)
                if stage == "warm up":
                    if i[1] == 0:
                        pe.wait_ge(k_id, 1)
                    for n in range(WARM_UP[i[1]]):
                        pe.matmul(ps_g[:, 0:P], ident[:], ident[:], start=True, stop=True)
                if stage == "turn":
                    wait(pe, s_lo, i)
                    wait(pe, s_od, (i + 1) // PER_B)
                    if i == CHUNKS:
                        pe.wait_ge(s_x2, CHUNKS - 4)
                    for n in range(NT):
                        pe.wait_ge(s_xn, NT * i + n + 1)
                        ins = pe.transpose(ps_t[:, n * P:(n + 1) * P], xn[:, i % 2, n], ident[:])
                    ins.then_inc(s_xt, 1)
                    if i == 0:
                        for j in range(LORA):
                            ins = pe.matmul(ps_m[:, j * D:(j + 1) * D], ident[:, 2 * j + 1:2 * j + 2].to_broadcast([P, P]),
                                            xn[:, 0, 0], start=True, stop=True)
                        ins.then_inc(k_sel, 1)
                if stage == "aturn":
                    wait(pe, a_lo, i)
                    if i == 0:
                        pe.wait_ge(s_w1r, LORA)
                    for n in range(NT):
                        pe.wait_ge(a_xn, NT * i + n + 1)
                        ins = pe.transpose(ps_m[:, n * P:(n + 1) * P], xa[:, i, n], ident[:])
                    ins.then_inc(a_xt, 1)
                if stage == "up":
                    f, j = i
                    if j == 0:
                        pe.wait_ge(s_lo, f + 1)
                        if f == CHUNKS:
                            pe.wait_ge(s_sub, 2 * CHUNKS)
                    pe.wait_ge(s_w1, LORA * (f // PER_B) + j + 1)
                    wait(pe, s_gelu, HB * f + j - 1)
                    blk, w = slice(j * P, (j + 1) * P), f // PER_B % 2
                    pe.matmul(ps_h[j % 2], w1h[:, w, blk], xh[:, f % 2], start=True, stop=False)
                    pe.matmul(ps_h[j % 2], w1h[:, w, blk], xl[:, f % 2], start=False, stop=False)
                    pe.matmul(ps_h[j % 2], w1l[:, w, blk], xh[:, f % 2], start=False, stop=True).then_inc(s_u, 1)
                if stage == "down":
                    f, n = i
                    if n == 0:
                        pe.wait_ge(s_gelu, HB * (f + 1))
                        pe.wait_ge(s_w2, f // PER_B + 1)
                        wait(pe, s_x1, min(f - 1, CHUNKS))
                        wait(pe, s_x3, f - 1 - CHUNKS)
                    y = ps_g if f == FC - 1 and n >= NT // 2 else ps_y[f % 2]
                    for j in range(HB):
                        ins = pe.matmul(y[:, n * P:(n + 1) * P], gl[:, f % 2, j, n * P:(n + 1) * P], w2e[:, f // PER_B % 2, j],
                                        start=(j == 0), stop=(j == HB - 1))
                    ins.then_inc(s_d, 1)
                if stage == "qk":
                    a, n = i
                    if n == 0:
                        pe.wait_ge(a_lo, a + 1)
                        if a == 0:
                            pe.wait_ge(s_gelu, HB * CHUNKS)
                            pe.wait_ge(k_wal, 1)
                    if a == 0 and n >= 2:
                        pe.wait_ge(s_x1, CHUNKS - 1 + n - 2)
                    if n % 2 == 0:
                        wait(pe, s_sub, 2 * a + n // 2 - 1)
                    to = quad[:, n]
                    tile = slice(n * P, (n + 1) * P)
                    pe.matmul(to, xah[:, a, tile], wah[:], start=True, stop=False)
                    pe.matmul(to, xah[:, a, tile], wal[:], start=False, stop=False)
                    pe.matmul(to, xal[:, a, tile], wah[:], start=False, stop=True).then_inc(s_qk, 1)
                if stage == "qturn":
                    pe.wait_ge(s_qn, i + 1)
                    wait(pe, s_qte, i)
                    for n in range(NT):
                        ins = pe.transpose(ps_r[:, n * P:(n + 1) * P], qn[:, i % 2, n], ident[:])
                    ins.then_inc(s_qt, 1)
                if stage == "gram":
                    k = i % PER_B
                    pe.wait_ge(s_exp, 2 * i + 2)
                    if i == 0:
                        pe.wait_ge(k_wv2, 1)
                    if k == 0:
                        wait(pe, m_gs, i // PER_B)
                    for n in range(NT):
                        ins = pe.matmul(ps_g[:, 0:D], qk[:, i % 2, n, 1, :], xa[:, i, n],
                                        start=(k == 0 and n == 0), stop=(k == PER_B - 1 and n == NT - 1))
                    ins.then_inc(s_g, 1)
                if stage == "mix":
                    b, k = i
                    if k == 0:
                        pe.wait_ge(m_gs, b + 1)
                        pe.wait_ge(a_lo, CHUNKS)
                        if b == NB - 1:
                            pe.wait_ge(s_x2, PER_B * b)
                        pe.transpose(ps_m[:, 0:D], gs[:], ident[:]).then_inc(m_gtp, 1)
                    if k == 1:
                        pe.wait_ge(m_gt, b + 1)
                        pe.matmul(ps_m[:, D:2 * D], gt[:], wv2[:], start=True, stop=True).then_inc(m_kv, 1)
                    if k == 2:
                        pe.wait_ge(m_kvm, b + 1)
                        pe.transpose(ps_m[:, 2 * D:3 * D], kvm[:], ident[:]).then_inc(m_ktp, 1)
                    if k == 3:
                        pe.wait_ge(m_kt, b + 1)
                        pe.matmul(ps_m[:, 3 * D:4 * D], kvt[:], wa[:, 3], start=True, stop=True).then_inc(m_mp, 1)
                if stage == "o":
                    pe.wait_ge(m_mo, i // PER_B + 1)
                    pe.wait_ge(s_qte, i + 1)
                    wait(pe, s_x2, i)
                    for n in range(NT):
                        ins = pe.matmul(ps_o[i][:, n * P:(n + 1) * P], qt[:, i % 4, n * P:(n + 1) * P], mo[:],
                                        start=True, stop=True)
                    ins.then_inc(s_o, 1)


def kernel(**inputs):
    import numpy as _np
    import concourse.bacc as _bacc
    from concourse import mybir as _mybir
    from concourse.bass_utils import run_bass_kernel_spmd as _run

    x, wq, bq, wk, bk, wv, bv, wo, bo, r = [_np.asarray(inputs["L0_attn_" + n]) for n in (
        "x", "Wq", "bq", "Wk", "bk", "Wv", "bv", "Wo", "bo", "R")]
    w1, b1, w2, b2, scale = [_np.asarray(inputs["L0_ffn_" + n]) for n in ("W1", "b1", "W2", "b2", "scale")]
    laid_out = {
        "x": x,
        "w1t": w1.T,
        "w2t": w2.T.reshape(HB, P, D).transpose(1, 0, 2),
        "wa": _np.stack([wq, wk, wv, wo.T], axis=1),
        "cols": _np.concatenate([b1.reshape(HB, P), _np.stack([bq, bk, bv])]).T,
        "rows": _np.concatenate([b2, bo, scale.reshape(1)]),
        "r": r,
    }
    nc = _bacc.Bacc("TRN2", target_bir_lowering=False, num_devices=1)
    arrays, args = {}, []
    for name, a in laid_out.items():
        a = _np.ascontiguousarray(a)
        arrays[f"in_{name}_dram"] = a
        args.append(nc.dram_tensor(f"in_{name}_dram", a.shape, _mybir.dt.from_np(a.dtype), kind="ExternalInput").ap())
    args.append(nc.dram_tensor("out_0_dram", (NB, SEQ, D), _mybir.dt.float32, kind="ExternalOutput").ap())
    args.append(nc.dram_tensor("token_rows", (2 * NB, 4 * LORA, D), _mybir.dt.float32, kind="Internal").ap())
    build(nc, *args)
    result = _run(nc, [arrays], core_ids=[0])
    return result.results[0]["out_0_dram"]
```

```python
import numpy as np
from contextlib import ExitStack

import concourse.bass as bass
from concourse import mybir

ALU = mybir.AluOpType
ACT = mybir.ActivationFunctionType
AX = mybir.AxisListType
F32 = mybir.dt.float32
F32R = mybir.dt.float32r

P = 128
D = 128
H = 512
NB, SEQ = 4, 1024
HEADS, HD = 16, 8
TOK = 512
NT = TOK // P
CHUNKS = NB * SEQ // TOK
PER_B = SEQ // TOK
HB = H // P
LORA = 4
LN_EPS, Z_EPS = 1e-5, 1e-8
WARM_UP = (11, 4)
SHIFT = 0.125
FC = 2 * CHUNKS


TIMES = {
    "sp": (
        {
            "rows": (-0.84, None),
        },
        {
        },
        {
            "rows": (-0.88, None), "down 3": (2.45, 2.43),
        },
    ),
    "pool": (
        {
            "stats": (-2.74, -3.73), "norm": (-0.77, 0.15), "w2": (-0.75, None), "astats": (3.24, 2.28),
            "anorm": (9.29, 8.79),
        },
        {
            "z": (3.3, 2.34),
        },
        {
            "stats": (-0.68, -1.2), "norm": (-0.65, 0.33), "w2": (1.31, None),
        },
    ),
    "act": (
        {
            "turn": (-0.62, -1.1), "up 0": (0.19, -0.18), "up 1": (0.33, -0.17), "load": (0.18, None),
            "up 2": (0.66, 0.39), "up 3": (0.81, 0.4), "split weights": (3.24, None), "anorm": (3.46, 3.85),
            "aturn": (4.84, 4.41),
        },
        {
            "feat 0": (0.34, 0.3), "feat 1": (0.96, 0.47), "exp 0": (1.35, 1.07), "exp 1": (1.42, 1.86),
            "gram": (None, 2.46), "qturn": (3.48, 4.43),
        },
        {
            "turn": (0.87, 0.49), "up 0": (1.44, 0.52), "up 1": (1.45, 0.53), "up 2": (1.5, 1.88),
            "up 3": (1.51, 1.89),
        },
    ),
    "dve": (
        {
            "stats": (-1.91, -2.53), "moments": (-1.9, -2.52), "norm": (-1.13, -2.1), "scale": (-1.14, None),
            "turn": (-0.39, -0.92), "odd": (-0.44, None), "w1": (-0.22, None), "constants": (1.62, None),
            "down 3": (2.12, 1.86), "astats": (2.49, 1.88), "amoments": (2.89, 3.11), "split weights": (3.57, None),
            "aturn": (4.91, 5.13),
        },
        {
            "head sums 0": (0.5, -0.02), "feat 0": (0.74, 0.67), "head sums 1": (0.95, 1.14),
            "feat 1": (0.97, 1.31), "z sums": (2.12, 1.92), "z eps": (2.28, 1.94), "z": (2.44, 1.96),
            "mix 0": (None, 3.51), "mix 1": (None, 3.93), "o": (4.99, 5.15),
        },
        {
            "stats": (-1.0, -0.48), "moments": (-0.97, -0.05), "norm": (-0.32, -0.02), "turn": (0.94, 0.02),
            "odd": (0.53, None), "w1": (0.97, None), "down 3": (3.01, 3.96),
        },
    ),
    "pe": (
        {
            "turn": (-0.89, -1.24), "warm up 0": (-1.13, None), "warm up 1": (-0.9, None), "up 0": (0.0, 0.0),
            "up 1": (0.14, 0.07), "up 2": (0.48, 0.09), "up 3": (0.55, 0.1), "down 0": (1.08, 0.8),
            "down 1": (1.12, 0.9), "down 2": (1.13, 1.29), "down 3": (1.66, 1.56), "split weights": (1.94, None),
            "aturn": (4.57, 4.14),
        },
        {
            "qk 0": (-0.22, 0.0), "qk 1": (-0.21, 0.01), "qk 2": (0.59, 0.16), "qk 3": (0.6, 0.17),
            "gram": (2.58, 2.15), "mix 0": (None, 2.8), "qturn": (3.18, 3.63), "mix 1": (None, 3.61),
            "o": (5.02, 4.23),
        },
        {
            "turn": (-0.63, 0.19), "up 0": (1.16, 0.25), "up 1": (1.17, 0.27), "up 2": (1.2, 0.81),
            "up 3": (1.22, 0.82), "down 0": (1.26, 1.64), "down 1": (1.28, 2.03), "down 2": (1.83, 2.21),
            "down 3": (2.62, 2.24),
        },
    ),
}
APART = {
    ("dve", "head sums", (2, 0)): 0.43,
    ("dve", "z sums", 7): 2.04,
    ("dve", "z eps", 1): 1.96,
    ("dve", "z eps", 7): 2.69,
    ("dve", "z", 1): 2.66,
    ("dve", "z", 7): 3.16,
    ("dve", "stats", 8): -2.28,
    ("dve", "moments", 8): -1.17,
    ("act", "anorm", 5): 3.35,
    ("act", "exp", (0, 0)): 0.76,
}


def work():
    for stage in ("load", "scale", "constants", "split weights"):
        yield stage, 0, 0, 0
    for k in range(2):
        yield "warm up", (0, k), 0, 0
    for f in range(FC):
        phase, step = (0, f) if f < CHUNKS else (2, f + CHUNKS)
        for stage in ("stats", "moments", "norm", "turn"):
            yield stage, f, phase, step
        if f % PER_B == 0:
            for stage in ("rows", "odd", "w1", "w2"):
                yield stage, f // PER_B, phase, step
        for j in range(HB):
            yield "up", (f, j), phase, step
        for n in range(NT):
            yield "down", (f, n), phase, step
    for a in range(CHUNKS):
        for stage in ("astats", "amoments", "anorm", "aturn"):
            yield stage, a, 0, a
        for n in range(NT):
            yield "qk", (a, n), 1, CHUNKS + a
        for p in range(2):
            yield "head sums", (a, p), 1, CHUNKS + a
            yield "feat", (a, p), 1, CHUNKS + a
            yield "exp", (a, p), 1, CHUNKS + a
        for stage in ("z sums", "z eps", "z", "gram", "qturn", "o"):
            yield stage, a, 1, CHUNKS + a
        if a % PER_B == PER_B - 1:
            for k in range(2):
                yield "mix", (a // PER_B, k), 1, CHUNKS + a


def plan(engine):
    placed = []
    for stage, i, phase, step in work():
        name = f"{stage} {i[1]}" if isinstance(i, tuple) else stage
        time = TIMES[engine][phase].get(name, (None, None))[step % 2]
        if time is not None:
            placed.append((step + APART.get((engine, stage, i), time), stage, i))
    placed.sort(key=lambda p: p[0])
    return [(stage, i) for _, stage, i in placed]


def stats(dve, i, x, bst, s_bst, s_mv):
    if i >= 2:
        dve.wait_ge(s_mv, i - 1)
    for n in range(NT):
        ins = dve.bn_stats(bst[:, i % 2, n], x[:, n])
    ins.then_inc(s_bst, 1)


def moments(dve, i, bst, mv, s_bst, s_mv, s_rstd, s_xn):
    dve.wait_ge(s_bst, i + 1)
    if i >= 2:
        dve.wait_ge(s_rstd, i - 1)
        dve.wait_ge(s_xn, NT * (i - 1))
    for n in range(NT):
        ins = dve.bn_aggr(mv[:, i % 2, n], bst[:, i % 2, n])
    ins.then_inc(s_mv, 1)


def inverse_root(pool, i, mv, veps, rstd, mhalf, s_mv, s_veps, s_rstd):
    pool.wait_ge(s_mv, i + 1)
    pool.tensor_scalar(veps[:, i % 2], mv[:, i % 2, :, 1], LN_EPS, None, ALU.add).then_inc(s_veps, 1)
    pool.wait_ge(s_veps, i + 1)
    pool.tensor_tensor(rstd[:, i % 2], veps[:, i % 2], mhalf[:], ALU.pow).then_inc(s_rstd, 1)


def build(nc, x, w1t_in, w2t_in, wa_in, cols_in, rows_in, r_in, out, token_rows):
    ctx = ExitStack()
    with ctx:
        def sb(name, shape, dt=F32):
            return ctx.enter_context(nc.sbuf_tensor(name, shape, dt))

        def sem(name):
            return ctx.enter_context(nc.semaphore(name))

        X = sb("X", [P, 3 * CHUNKS, NT, D])
        bst = sb("bst", [P, 2, NT, 6])
        mv = sb("mv", [P, 2, NT, 2])
        veps = sb("veps", [P, 2, NT])
        rstd = sb("rstd", [P, 2, NT])
        mhalf = sb("mhalf", [P, NT])
        table = sb("table", [P, 1])
        xn = sb("xn", [P, 2, NT, D])
        xh = sb("xh", [P, 2, TOK], F32R)
        xl = sb("xl", [P, 2, TOK], F32R)
        abst = sb("abst", [P, 2, NT, 6])
        amv = sb("amv", [P, 2, NT, 2])
        aveps = sb("aveps", [P, 2, NT])
        arstd = sb("arstd", [P, 2, NT])
        amr = sb("amr", [P, 2, NT])
        anmr = sb("anmr", [P, 2, NT])
        xa = sb("xa", [P, CHUNKS, NT, D])
        xah = sb("xah", [P, CHUNKS, TOK], F32R)
        xal = sb("xal", [P, CHUNKS, TOK], F32R)
        gl = sb("gl", [P, 2, HB, TOK])
        w1t = sb("w1t", [P, H])
        w2n = sb("w2n", [P, HB, D])
        w2t = sb("w2t", [P, HB, D])
        ev = sb("ev", [P, 2 * LORA, D])
        od = sb("od", [P, 2 * LORA])
        scl = sb("scl", [P, 2 * LORA])
        w1r = sb("w1r", [P, LORA, D])
        w1h = sb("w1h", [P, 2, H], F32R)
        w1l = sb("w1l", [P, 2, H], F32R)
        w2m = sb("w2m", [P, LORA, D])
        w2e = sb("w2e", [P, 2, HB, D])
        cols = sb("cols", [P, HB + 3])
        rows = sb("rows", [P, 2 * D + 1])
        b2h = sb("b2h", [P, D])
        ident = sb("ident", [P, P])
        bd = sb("bd", [P, HEADS, HD])
        rrep = sb("rrep", [P, HD])
        irbd = sb("irbd", [P, 2, P])
        wa = sb("wa", [P, 4, D])
        wsum = sb("wsum", [P, 3])
        vd = sb("vd", [P, 3])
        vs = sb("vs", [P, 3])
        wb = sb("wb", [P, 3, D])
        wv2 = sb("wv2", [P, D])
        wah = sb("wah", [P, TOK], F32R)
        wal = sb("wal", [P, TOK], F32R)
        sq = sb("sq", [P, 2, 4, P])
        s8 = sb("s8", [P, 2, 4 * HEADS])
        ex = sb("ex", [P, 2, 4, P])
        qk = sb("qk", [P, 2, NT, 2, P])
        zs = sb("zs", [P, 2, NT * HEADS])
        zr = sb("zr", [P, NT, HEADS])
        qn = sb("qn", [P, 2, NT, P])
        qt = sb("qt", [P, 4, TOK])
        gs = sb("gs", [P, D])
        kvm = sb("kvm", [P, D])
        mo = sb("mo", [P, D])

        def bank(name):
            return ctx.enter_context(nc.psum_tensor(name, [P, TOK], F32))

        ps_t = bank("ps_t")
        quad = ctx.enter_context(nc.psum_tensor("quad", [P, NT, TOK], F32))
        ps_h = [quad[:, 0], quad[:, 1]]
        ps_y = [quad[:, 2], quad[:, 3]]
        ps_g, ps_r, ps_m = bank("ps_g"), bank("ps_r"), bank("ps_m")
        ps_o = [ps_t] * (CHUNKS - 4) + [ps_m] * 3 + [ps_r]

        ld_x = [sem(f"ld_x{c}") for c in range(CHUNKS)]
        ld_w1, ld_w2, ld_cols, ld_rows, ld_wa, ld_r = [sem(f"ld_{n}") for n in ("w1", "w2", "cols", "rows", "wa", "r")]
        k_exp, k_sel, k_zero, k_id, k_bd0, k_bd1, k_bd = [sem(f"k_{n}") for n in ("exp", "sel", "zero", "id", "bd0", "bd1", "bd")]
        k_scl, k_b2h, k_w2t, k_rbd, k_wsum, k_vd = [sem(f"k_{n}") for n in ("scl", "b2h", "w2t", "rbd", "wsum", "vd")]
        k_vs, k_wb, k_war, k_wv, k_wah, k_wal, k_wv2 = [sem(f"k_{n}") for n in ("vs", "wb", "war", "wv", "wah", "wal", "wv2")]
        s_bst, s_mv, s_veps, s_rstd, s_xn, s_xt, s_hi, s_lo, s_xb = [
            sem(f"s_{n}") for n in ("bst", "mv", "veps", "rstd", "xn", "xt", "hi", "lo", "xb")]
        s_u, s_gelu, s_d = sem("s_u"), sem("s_gelu"), sem("s_d")
        s_x1, s_x3 = sem("s_x1"), sem("s_x3")
        s_rows, s_ev = sem("s_rows"), sem("s_ev")
        s_od, s_w1r, s_w1h, s_w1, s_w2m, s_w2 = [sem(f"s_{n}") for n in ("od", "w1r", "w1h", "w1", "w2m", "w2")]
        a_bst, a_mv, a_veps, a_rstd, a_mr, a_nmr, a_xn, a_xt, a_hi, a_lo, a_xb = [
            sem(f"a_{n}") for n in ("bst", "mv", "veps", "rstd", "mr", "nmr", "xn", "xt", "hi", "lo", "xb")]
        s_qk = sem("s_qk")
        s_sq, s_red, s_sub, s_exp = [sem(f"s_{n}") for n in ("sq", "red", "sub", "exp")]
        s_zs, s_ze, s_zr, s_qn, s_qt, s_qte, s_g, s_o, s_x2 = [
            sem(f"s_{n}") for n in ("zs", "ze", "zr", "qn", "qt", "qte", "g", "o", "x2")]
        m_gs, m_kv, m_kvm, m_mp, m_mo = [sem(f"m_{n}") for n in ("gs", "kv", "kvm", "mp", "mo")]
        s_out = sem("s_out")

        def chunk_of(t, c):
            flat = t.rearrange("b s d -> (b s) d")
            return flat[c * TOK:(c + 1) * TOK, :].rearrange("(n p) d -> p n d", p=P)

        def wait(eng, s, n):
            if n > 0:
                eng.wait_ge(s, n)

        def xslot(f):
            return f if f < CHUNKS else f + CHUNKS

        def halves(p, which):
            return quad[:, 2 * p:2 * p + 2, :].rearrange("p n (k w d) -> p w (n k) d", k=2, w=2)[:, which]

        def flat(t):
            return t.rearrange("p n d -> p (n d)")

        def heads(t):
            return t.rearrange("p n (h d) -> p n h d", h=HEADS)

        block = ctx.enter_context(nc.Block())

        @block.sync
        def _(sp):
            sp.dma_start(X[:, 0], chunk_of(x, 0)).then_inc(ld_x[0], 16)
            sp.dma_start(X[:, 1], chunk_of(x, 1)).then_inc(ld_x[1], 16)
            sp.dma_start(rows[:], rows_in.partition_broadcast(P)).then_inc(ld_rows, 16)
            sp.dma_start(w1t[:], w1t_in).then_inc(ld_w1, 16)
            sp.dma_start(cols[:], cols_in).then_inc(ld_cols, 16)
            sp.dma_start(w2n[:], w2t_in).then_inc(ld_w2, 16)
            sp.dma_start(X[:, 2], chunk_of(x, 2)).then_inc(ld_x[2], 16)
            sp.dma_start(wa[:], wa_in).then_inc(ld_wa, 16)
            sp.dma_start(rrep[:], r_in.partition_broadcast(HEADS)).then_inc(ld_r, 16)
            for stage, i in plan("sp"):
                if stage == "rows":
                    sp.wait_ge(s_xn, NT * PER_B * i + 1)
                    sp.dma_start(token_rows[i], xn[1:1 + 4 * LORA, 0, 0, :]).then_inc(s_rows, 16)
                    sp.wait_ge(s_rows, 16 * (i + 1))
                    wait(sp, s_w1r, LORA * i)
                    wait(sp, s_w2m, i)
                    even = token_rows[i].rearrange("(n two) d -> two n d", two=2)[0]
                    sp.dma_start(ev[:], even.partition_broadcast(P)).then_inc(s_ev, 16)
                    if i == 0:
                        for c in range(3, CHUNKS):
                            sp.dma_start(X[:, c], chunk_of(x, c)).then_inc(ld_x[c], 16)
                if stage == "down" and i[0] >= CHUNKS and i[1] == NT - 1:
                    c = i[0] - CHUNKS
                    parts = 2 if c == CHUNKS - 1 else 1
                    for h in range(parts):
                        tiles = slice(NT // parts * h, NT // parts * (h + 1))
                        sp.wait_ge(s_x3, c + h + 1)
                        sp.dma_start(chunk_of(out, c)[:, tiles], X[:, xslot(i[0]), tiles]).then_inc(s_out, 16)
            sp.wait_ge(s_out, 16 * (CHUNKS + 1))

        @block.gpsimd
        def _(pool):
            pool.memset(mhalf[:], -0.5).then_inc(k_exp, 1)
            pool.memset(ident[:], 0.0).then_inc(k_zero, 1)
            pool.wait_ge(k_zero, 1)
            pool.affine_select(out=ident[:], in_=ident[:], compare_op=ALU.not_equal, fill=1.0, base=0,
                               pattern=[[-1, P]], channel_multiplier=1).then_inc(k_id, 1)
            pool.memset(irbd[:, 0], 0.0).then_inc(k_zero, 1)
            pool.wait_ge(k_zero, 2)
            pool.affine_select(out=irbd[:, 0], in_=irbd[:, 0], compare_op=ALU.not_equal, fill=1.0, base=0,
                               pattern=[[-1, P]], channel_multiplier=1).then_inc(k_id, 1)
            pool.memset(bd[:], 1.0).then_inc(k_bd0, 1)
            pool.wait_ge(k_bd0, 1)
            pool.affine_select(out=bd[:], in_=bd[:], compare_op=ALU.is_ge, fill=0.0, base=0,
                               pattern=[[-HD, HEADS], [0, HD]], channel_multiplier=1).then_inc(k_bd1, 1)
            pool.wait_ge(k_bd1, 1)
            pool.affine_select(out=bd[:], in_=bd[:], compare_op=ALU.is_ge, fill=0.0, base=HD - 1,
                               pattern=[[HD, HEADS], [0, HD]], channel_multiplier=-1).then_inc(k_bd, 1)
            for stage, i in plan("pool"):
                if stage == "stats":
                    if i == 0:
                        pool.wait_ge(k_exp, 1)
                    wait(pool, s_xn, NT * (i - 1))
                    inverse_root(pool, i, mv, veps, rstd, mhalf, s_mv, s_veps, s_rstd)
                if stage == "astats":
                    wait(pool, a_xn, NT * (i - 1))
                    inverse_root(pool, i, amv, aveps, arstd, mhalf, a_mv, a_veps, a_rstd)
                    pool.wait_ge(a_rstd, i + 1)
                    pool.tensor_tensor(amr[:, i % 2], amv[:, i % 2, :, 0], arstd[:, i % 2], ALU.mult).then_inc(a_mr, 1)
                    pool.wait_ge(a_mr, i + 1)
                    pool.tensor_scalar(anmr[:, i % 2], amr[:, i % 2], -1.0, SHIFT, ALU.mult, ALU.add).then_inc(a_nmr, 1)
                if stage == "norm":
                    pool.wait_ge(s_xn, NT * (i + 1))
                    if i == 0:
                        pool.wait_ge(k_b2h, 1)
                    pool.tensor_tensor(X[:, xslot(i)], X[:, xslot(i)], b2h[:].unsqueeze(1).to_broadcast([P, NT, D]),
                                       ALU.add).then_inc(s_xb, 1)
                if stage == "anorm":
                    pool.wait_ge(a_xn, NT * (i + 1))
                    pool.tensor_tensor(X[:, CHUNKS + i], X[:, CHUNKS + i],
                                       rows[:, D:2 * D].unsqueeze(1).to_broadcast([P, NT, D]), ALU.add).then_inc(a_xb, 1)
                if stage == "w2":
                    pool.wait_ge(s_ev, 16 * (i + 1))
                    pool.wait_ge(s_od, i + 1)
                    wait(pool, s_w2, i)
                    pool.tensor_tensor(w2m[:], ev[:, LORA:2 * LORA],
                                       od[:, LORA:2 * LORA].unsqueeze(2).to_broadcast([P, LORA, D]),
                                       ALU.mult).then_inc(s_w2m, 1)
                    pool.wait_ge(s_w2m, i + 1)
                    if i == 0:
                        pool.wait_ge(k_w2t, 1)
                    wait(pool, s_d, NT * PER_B * (i - 1))
                    pool.tensor_tensor(w2e[:, i % 2], flat(w2m[:]).rearrange("p (o k) -> p k o", k=HB),
                                       w2t[:], ALU.add).then_inc(s_w2, 1)
                if stage == "z":
                    pool.wait_ge(s_zr, i + 1)
                    wait(pool, s_qt, i - 1)
                    pool.tensor_tensor(heads(qn[:, i % 2]), heads(qk[:, i % 2, :, 0, :]),
                                       zr[:].unsqueeze(3).to_broadcast([P, NT, HEADS, HD]),
                                       ALU.mult).then_inc(s_qn, 1)

        @block.scalar
        def _(act):
            act.wait_ge(k_exp, 1)
            act.activation(table[:], mhalf[:, 0:1], ACT.Gelu)
            for stage, i in plan("act"):
                if stage == "load":
                    act.wait_ge(ld_w2, 16)
                    act.activation(flat(w2t[:]), flat(w2n[:]), ACT.Copy, scale=0.5).then_inc(k_w2t, 1)
                if stage == "split weights":
                    act.wait_ge(k_war, 1)
                    act.activation(wah[:], ps_r[:], ACT.Copy).then_inc(k_wah, 1)
                if stage == "turn":
                    act.wait_ge(s_xt, i + 1)
                    wait(act, s_u, HB * (i - 1))
                    act.activation(xh[:, i % 2], ps_t[:], ACT.Copy).then_inc(s_hi, 1)
                if stage == "aturn":
                    act.wait_ge(a_xt, i + 1)
                    act.activation(xah[:, i], ps_m[:], ACT.Copy).then_inc(a_hi, 1)
                if stage == "anorm":
                    act.wait_ge(a_nmr, i + 1)
                    for n in range(NT):
                        act.activation(xa[:, i, n], X[:, CHUNKS + i, n], ACT.Identity, bias=anmr[:, i % 2, n:n + 1],
                                       scale=arstd[:, i % 2, n:n + 1]).then_inc(a_xn, 1)
                if stage == "up":
                    f, j = i
                    act.wait_ge(s_u, HB * f + j + 1)
                    if j == 0:
                        wait(act, s_d, NT * (f - 1))
                        if f == 0:
                            act.wait_ge(ld_cols, 16)
                    act.activation(gl[:, f % 2, j], ps_h[j % 2], ACT.Gelu, bias=cols[:, j:j + 1]).then_inc(s_gelu, 1)
                if stage == "feat":
                    a, p = i
                    act.wait_ge(s_qk, NT * a + 2 * p + 2)
                    wait(act, s_red, 2 * a + p - 1)
                    act.activation(sq[:, p], halves(p, 0), ACT.Square, scale=0.25).then_inc(s_sq, 1)
                if stage == "exp":
                    a, p = i
                    act.wait_ge(s_sub, 2 * a + p + 1)
                    if p == 0:
                        wait(act, s_g, a - 1)
                        wait(act, s_qn, a - 1)
                    act.activation(qk[:, a % 2, 2 * p:2 * p + 2].rearrange("p n k d -> p (n k) d"), ex[:, p],
                                   ACT.Exp).then_inc(s_exp, 1)
                if stage == "qturn":
                    act.wait_ge(s_qt, i + 1)
                    wait(act, s_o, i - 3)
                    act.activation(qt[:, i % 4], ps_r[:], ACT.Copy).then_inc(s_qte, 1)
                if stage == "gram" and i % PER_B == PER_B - 1:
                    b = i // PER_B
                    act.wait_ge(s_g, i + 1)
                    wait(act, m_kv, b)
                    act.activation(gs[:], ps_g[:, 0:D], ACT.Copy).then_inc(m_gs, 1)

        @block.vector
        def _(dve):
            for stage, i in plan("dve"):
                if stage == "constants":
                    dve.wait_ge(k_bd, 1)
                    dve.wait_ge(ld_r, 16)
                    dve.scalar_tensor_tensor(out=irbd[:, 1].rearrange("p (h d) -> p h d", h=HEADS),
                                             in0=rrep[:].unsqueeze(1).to_broadcast([P, HEADS, HD]),
                                             scalar=float(HD) ** -0.5, in1=bd[:], op0=ALU.mult,
                                             op1=ALU.mult).then_inc(k_rbd, 1)
                    dve.wait_ge(ld_wa, 16)
                    dve.tensor_reduce(wsum[:], wa[:, 0:3], AX.X, ALU.add).then_inc(k_wsum, 1)
                    dve.wait_ge(k_wsum, 1)
                    dve.wait_ge(ld_cols, 16)
                    dve.scalar_tensor_tensor(out=vd[:], in0=wsum[:], scalar=-SHIFT, in1=cols[:, HB:HB + 3],
                                             op0=ALU.mult, op1=ALU.add).then_inc(k_vd, 1)
                    dve.wait_ge(k_vd, 1)
                    dve.tensor_scalar(vs[:], vd[:], 1.0 / (D * SHIFT), None, ALU.mult).then_inc(k_vs, 1)
                    dve.wait_ge(k_vs, 1)
                    for k in range(3):
                        ins = dve.tensor_scalar(wb[:, k], wa[:, k], vs[:, k:k + 1], None, ALU.add)
                    ins.then_inc(k_wb, 1)
                if stage == "split weights":
                    dve.wait_ge(k_wah, 1)
                    dve.tensor_tensor(wal[:], ps_r[:], wah[:].bitcast(F32), ALU.subtract).then_inc(k_wal, 1)
                    dve.wait_ge(k_wv, 1)
                    dve.tensor_copy(wv2[:], ps_g[:, 0:D]).then_inc(k_wv2, 1)
                if stage == "stats":
                    if i < CHUNKS:
                        dve.wait_ge(ld_x[i], 16)
                    else:
                        dve.wait_ge(s_x2, i - CHUNKS + 1)
                    stats(dve, i, X[:, xslot(i)], bst, s_bst, s_mv)
                if stage == "moments":
                    moments(dve, i, bst, mv, s_bst, s_mv, s_rstd, s_xn)
                if stage == "norm":
                    dve.wait_ge(s_rstd, i + 1)
                    wait(dve, s_xt, i - 1)
                    wait(dve, s_rows, 16 * (i // PER_B))
                    for n in range(NT):
                        dve.tensor_scalar(xn[:, i % 2, n], X[:, xslot(i), n], mv[:, i % 2, n, 0:1],
                                          rstd[:, i % 2, n:n + 1], ALU.subtract, ALU.mult).then_inc(s_xn, 1)
                if stage == "scale":
                    dve.wait_ge(ld_rows, 16)
                    dve.tensor_scalar(b2h[:], rows[:, 0:D], 0.5, None, ALU.mult).then_inc(k_b2h, 1)
                    s = rows[:, 2 * D:2 * D + 1].to_broadcast([P, LORA])
                    dve.tensor_copy(scl[:, 0:LORA], s).then_inc(k_scl, 1)
                    dve.tensor_scalar(scl[:, LORA:], s, 0.5, None, ALU.mult).then_inc(k_scl, 1)
                if stage == "astats":
                    dve.wait_ge(s_x1, i + 1)
                    stats(dve, i, X[:, CHUNKS + i], abst, a_bst, a_mv)
                if stage == "amoments":
                    wait(dve, a_mr, i - 1)
                    moments(dve, i, abst, amv, a_bst, a_mv, a_rstd, a_xn)
                if stage == "turn":
                    dve.wait_ge(s_hi, i + 1)
                    wait(dve, s_u, HB * (i - 1))
                    dve.tensor_tensor(xl[:, i % 2], ps_t[:], xh[:, i % 2].bitcast(F32), ALU.subtract).then_inc(s_lo, 1)
                if stage == "odd":
                    dve.wait_ge(s_hi, PER_B * i + 1)
                    if i == 0:
                        dve.wait_ge(k_scl, 2)
                    wait(dve, s_w2m, i)
                    wait(dve, s_w1r, LORA * i)
                    dve.tensor_tensor(od[:], ps_t[:, 2:2 + 4 * LORA:2], scl[:], ALU.mult).then_inc(s_od, 1)
                if stage == "aturn":
                    dve.wait_ge(a_hi, i + 1)
                    dve.tensor_tensor(xal[:, i], ps_m[:], xah[:, i].bitcast(F32), ALU.subtract).then_inc(a_lo, 1)
                if stage == "w1":
                    dve.wait_ge(s_od, i + 1)
                    if i == 0:
                        dve.wait_ge(ld_w1, 16)
                        dve.wait_ge(k_sel, 1)
                    else:
                        dve.wait_ge(s_ev, 16 * (i + 1))
                        dve.wait_ge(s_w1, LORA * i)
                    even = ps_m[:].rearrange("p (j d) -> p j d", j=LORA) if i == 0 else ev
                    for j in range(LORA + 2):
                        if j < LORA:
                            dve.scalar_tensor_tensor(out=w1r[:, j], in0=even[:, j], scalar=od[:, j:j + 1],
                                                     in1=w1t[:, j * D:(j + 1) * D], op0=ALU.mult,
                                                     op1=ALU.add).then_inc(s_w1r, 1)
                        if 1 <= j <= LORA:
                            dve.wait_ge(s_w1r, LORA * i + j)
                            if j == 1:
                                wait(dve, s_u, HB * PER_B * (i - 1))
                            dve.tensor_copy(w1h[:, i % 2, (j - 1) * D:j * D], w1r[:, j - 1]).then_inc(s_w1h, 1)
                        if j >= 2:
                            blk = slice((j - 2) * D, (j - 1) * D)
                            dve.wait_ge(s_w1h, LORA * i + j - 1)
                            dve.tensor_tensor(w1l[:, i % 2, blk], w1r[:, j - 2], w1h[:, i % 2, blk].bitcast(F32),
                                              ALU.subtract).then_inc(s_w1, 1)
                if stage == "down" and i[1] == NT - 1:
                    f = i[0]
                    to = CHUNKS + f if f < CHUNKS else xslot(f)
                    dve.wait_ge(s_xb, f + 1)
                    parts = 2 if f == FC - 1 else 1
                    for h in range(parts):
                        tiles, part = NT // parts, TOK // parts
                        dve.wait_ge(s_d, NT * f + tiles * (h + 1))
                        dve.tensor_tensor(flat(X[:, to, tiles * h:tiles * (h + 1)]),
                                          (ps_g if h == 1 else ps_y[f % 2])[:, part * h:part * (h + 1)],
                                          flat(X[:, xslot(f), tiles * h:tiles * (h + 1)]), ALU.add).then_inc(
                            s_x1 if f < CHUNKS else s_x3, 1)
                if stage == "head sums":
                    a, p = i
                    wait(dve, s_sub, 2 * a + p - 1)
                    dve.wait_ge(s_sq, 2 * a + p + 1)
                    dve.tensor_reduce(s8[:, p], sq[:, p].rearrange("p u (h d) -> p (u h) d", h=HEADS),
                                      AX.X, ALU.add).then_inc(s_red, 1)
                if stage == "feat":
                    a, p = i
                    dve.wait_ge(s_red, 2 * a + p + 1)
                    wait(dve, s_exp, 2 * a + p - 1)
                    dve.tensor_tensor(heads(ex[:, p]), heads(halves(p, 1)),
                                      s8[:, p].rearrange("p (u h) -> p u h", u=4).unsqueeze(3).to_broadcast([P, 4, HEADS, HD]),
                                      ALU.subtract).then_inc(s_sub, 1)
                if stage == "z sums":
                    dve.wait_ge(s_exp, 2 * i + 2)
                    wait(dve, s_ze, i)
                    dve.tensor_reduce(zs[:, 0], heads(qk[:, i % 2, :, 0, :]), AX.X, ALU.add).then_inc(s_zs, 1)
                if stage == "z eps":
                    dve.wait_ge(s_zs, i + 1)
                    wait(dve, s_zr, i)
                    dve.tensor_scalar(zs[:, 1], zs[:, 0], Z_EPS, None, ALU.add).then_inc(s_ze, 1)
                if stage == "z":
                    dve.wait_ge(s_ze, i + 1)
                    wait(dve, s_qn, i)
                    dve.reciprocal(flat(zr[:]), zs[:, 1]).then_inc(s_zr, 1)
                if stage == "mix":
                    b, k = i
                    if k == 0:
                        dve.wait_ge(m_kv, b + 1)
                        dve.tensor_tensor(kvm[:], ps_m[:, 0:D], flat(bd[:]), ALU.mult).then_inc(m_kvm, 1)
                    if k == 1:
                        dve.wait_ge(m_mp, b + 1)
                        wait(dve, s_o, PER_B * b)
                        dve.tensor_copy(mo[:], ps_m[:, D:2 * D]).then_inc(m_mo, 1)
                if stage == "o":
                    dve.wait_ge(s_o, i + 1)
                    dve.wait_ge(a_xb, i + 1)
                    dve.tensor_tensor(flat(X[:, 2 * CHUNKS + i]), ps_o[i][:], flat(X[:, CHUNKS + i]),
                                      ALU.add).then_inc(s_x2, 1)

        @block.tensor
        def _(pe):
            for stage, i in plan("pe"):
                if stage == "split weights":
                    pe.wait_ge(k_wb, 1)
                    pe.wait_ge(k_id, 2)
                    pe.wait_ge(k_rbd, 1)
                    for k in range(2):
                        ins = pe.matmul(ps_r[:, 2 * k * D:2 * (k + 1) * D], wb[:, k], flat(irbd[:]), start=True, stop=True)
                    ins.then_inc(k_war, 1)
                    pe.transpose(ps_g[:, 0:D], wb[:, 2], ident[:]).then_inc(k_wv, 1)
                if stage == "warm up":
                    if i[1] == 0:
                        pe.wait_ge(k_id, 1)
                    for n in range(WARM_UP[i[1]]):
                        pe.matmul(ps_g[:, 0:P], ident[:], ident[:], start=True, stop=True)
                if stage == "turn":
                    wait(pe, s_lo, i)
                    wait(pe, s_od, (i + 1) // PER_B)
                    if i == CHUNKS:
                        pe.wait_ge(s_x2, CHUNKS - 4)
                    for n in range(NT):
                        pe.wait_ge(s_xn, NT * i + n + 1)
                        ins = pe.transpose(ps_t[:, n * P:(n + 1) * P], xn[:, i % 2, n], ident[:])
                    ins.then_inc(s_xt, 1)
                    if i == 0:
                        for j in range(LORA):
                            ins = pe.matmul(ps_m[:, j * D:(j + 1) * D], ident[:, 2 * j + 1:2 * j + 2].to_broadcast([P, P]),
                                            xn[:, 0, 0], start=True, stop=True)
                        ins.then_inc(k_sel, 1)
                if stage == "aturn":
                    wait(pe, a_lo, i)
                    if i == 0:
                        pe.wait_ge(s_w1r, LORA)
                    for n in range(NT):
                        pe.wait_ge(a_xn, NT * i + n + 1)
                        ins = pe.transpose(ps_m[:, n * P:(n + 1) * P], xa[:, i, n], ident[:])
                    ins.then_inc(a_xt, 1)
                if stage == "up":
                    f, j = i
                    if j == 0:
                        pe.wait_ge(s_lo, f + 1)
                        if f == CHUNKS:
                            pe.wait_ge(s_sub, 2 * CHUNKS)
                    pe.wait_ge(s_w1, LORA * (f // PER_B) + j + 1)
                    wait(pe, s_gelu, HB * f + j - 1)
                    blk, w = slice(j * P, (j + 1) * P), f // PER_B % 2
                    pe.matmul(ps_h[j % 2], w1h[:, w, blk], xh[:, f % 2], start=True, stop=False)
                    pe.matmul(ps_h[j % 2], w1h[:, w, blk], xl[:, f % 2], start=False, stop=False)
                    pe.matmul(ps_h[j % 2], w1l[:, w, blk], xh[:, f % 2], start=False, stop=True).then_inc(s_u, 1)
                if stage == "down":
                    f, n = i
                    if n == 0:
                        pe.wait_ge(s_gelu, HB * (f + 1))
                        pe.wait_ge(s_w2, f // PER_B + 1)
                        wait(pe, s_x1, min(f - 1, CHUNKS))
                        wait(pe, s_x3, f - 1 - CHUNKS)
                    y = ps_g if f == FC - 1 and n >= NT // 2 else ps_y[f % 2]
                    for j in range(HB):
                        ins = pe.matmul(y[:, n * P:(n + 1) * P], gl[:, f % 2, j, n * P:(n + 1) * P], w2e[:, f // PER_B % 2, j],
                                        start=(j == 0), stop=(j == HB - 1))
                    ins.then_inc(s_d, 1)
                if stage == "qk":
                    a, n = i
                    if n == 0:
                        pe.wait_ge(a_lo, a + 1)
                        if a == 0:
                            pe.wait_ge(s_gelu, HB * CHUNKS)
                            pe.wait_ge(k_wal, 1)
                    if a == 0 and n >= 2:
                        pe.wait_ge(s_x1, CHUNKS - 1 + n - 2)
                    if n % 2 == 0:
                        wait(pe, s_sub, 2 * a + n // 2 - 1)
                    to = quad[:, n]
                    tile = slice(n * P, (n + 1) * P)
                    pe.matmul(to, xah[:, a, tile], wah[:], start=True, stop=False)
                    pe.matmul(to, xah[:, a, tile], wal[:], start=False, stop=False)
                    pe.matmul(to, xal[:, a, tile], wah[:], start=False, stop=True).then_inc(s_qk, 1)
                if stage == "qturn":
                    pe.wait_ge(s_qn, i + 1)
                    wait(pe, s_qte, i)
                    for n in range(NT):
                        ins = pe.transpose(ps_r[:, n * P:(n + 1) * P], qn[:, i % 2, n], ident[:])
                    ins.then_inc(s_qt, 1)
                if stage == "gram":
                    k = i % PER_B
                    pe.wait_ge(s_exp, 2 * i + 2)
                    if i == 0:
                        pe.wait_ge(k_wv2, 1)
                    if k == 0:
                        wait(pe, m_gs, i // PER_B)
                    for n in range(NT):
                        ins = pe.matmul(ps_g[:, 0:D], xa[:, i, n], qk[:, i % 2, n, 1, :],
                                        start=(k == 0 and n == 0), stop=(k == PER_B - 1 and n == NT - 1))
                    ins.then_inc(s_g, 1)
                if stage == "mix":
                    b, k = i
                    if k == 0:
                        pe.wait_ge(m_gs, b + 1)
                        pe.wait_ge(a_lo, CHUNKS)
                        if b == NB - 1:
                            pe.wait_ge(s_x2, PER_B * b)
                        pe.matmul(ps_m[:, 0:D], wv2[:], gs[:], start=True, stop=True).then_inc(m_kv, 1)
                    if k == 1:
                        pe.wait_ge(m_kvm, b + 1)
                        pe.matmul(ps_m[:, D:2 * D], kvm[:], wa[:, 3], start=True, stop=True).then_inc(m_mp, 1)
                if stage == "o":
                    pe.wait_ge(m_mo, i // PER_B + 1)
                    pe.wait_ge(s_qte, i + 1)
                    wait(pe, s_x2, i)
                    for n in range(NT):
                        ins = pe.matmul(ps_o[i][:, n * P:(n + 1) * P], qt[:, i % 4, n * P:(n + 1) * P], mo[:],
                                        start=True, stop=True)
                    ins.then_inc(s_o, 1)


def kernel(**inputs):
    import numpy as _np
    import concourse.bacc as _bacc
    from concourse import mybir as _mybir
    from concourse.bass_utils import run_bass_kernel_spmd as _run

    x, wq, bq, wk, bk, wv, bv, wo, bo, r = [_np.asarray(inputs["L0_attn_" + n]) for n in (
        "x", "Wq", "bq", "Wk", "bk", "Wv", "bv", "Wo", "bo", "R")]
    w1, b1, w2, b2, scale = [_np.asarray(inputs["L0_ffn_" + n]) for n in ("W1", "b1", "W2", "b2", "scale")]
    laid_out = {
        "x": x,
        "w1t": w1.T,
        "w2t": w2.T.reshape(HB, P, D).transpose(1, 0, 2),
        "wa": _np.stack([wq, wk, wv, wo.T], axis=1),
        "cols": _np.concatenate([b1.reshape(HB, P), _np.stack([bq, bk, bv])]).T,
        "rows": _np.concatenate([b2, bo, scale.reshape(1)]),
        "r": r,
    }
    nc = _bacc.Bacc("TRN2", target_bir_lowering=False, num_devices=1)
    arrays, args = {}, []
    for name, a in laid_out.items():
        a = _np.ascontiguousarray(a)
        arrays[f"in_{name}_dram"] = a
        args.append(nc.dram_tensor(f"in_{name}_dram", a.shape, _mybir.dt.from_np(a.dtype), kind="ExternalInput").ap())
    args.append(nc.dram_tensor("out_0_dram", (NB, SEQ, D), _mybir.dt.float32, kind="ExternalOutput").ap())
    args.append(nc.dram_tensor("token_rows", (2 * NB, 4 * LORA, D), _mybir.dt.float32, kind="Internal").ap())
    build(nc, *args)
    result = _run(nc, [arrays], core_ids=[0])
    return result.results[0]["out_0_dram"]
```
